# Optimizing a Trainium2 kernel written in Bass

```python
import numpy as np
import jax
import jax.numpy as jnp

def _softmax(x, axis=-1):
    return jax.nn.softmax(x, axis=axis)

def _gelu(x):
    return jax.nn.gelu(x, approximate=True)

def _silu(x):
    return jax.nn.silu(x)

def _sigmoid(x):
    return jax.nn.sigmoid(x)

def _layernorm(x, axis=-1, eps=1e-05):
    m = jnp.mean(x, axis=axis, keepdims=True)
    v = jnp.var(x, axis=axis, keepdims=True)
    return (x - m) / jnp.sqrt(v + eps)

def _scatter_add(tgt, idx, src, axis=0):
    return tgt.at[idx].add(src)

def _segment_sum(src, seg, n):
    return jax.ops.segment_sum(src, seg, n)
kernel_name = 'mk_prb_d1_jaxref_r4_c800f6'

def setup_inputs(seed: int=0):
    np.random.seed(seed)
    _w = jnp.asarray

    def _L0_attn_setup():
        import jax, jax.numpy as jnp
        import numpy as np
        B, S, D = (2, 512, 256)
        N_HEADS, N_KV_HEADS = (16, 4)
        HEAD_DIM = D // N_HEADS
        KV_GROUPS = N_HEADS // N_KV_HEADS
        ROPE_BASE = 10000.0

        def _apply_rope(t, cos, sin):
            t1, t2 = jnp.split(t, 2, axis=-1)
            return jnp.concatenate([t1 * cos - t2 * sin, t1 * sin + t2 * cos], axis=-1)
        key = jax.random.key(seed)
        ks = jax.random.split(key, 5)
        s = 0.02
        return {'x': jax.random.normal(ks[0], (B, S, D), dtype=jnp.float32), 'wq': jax.random.normal(ks[1], (D, D), dtype=jnp.float32) * s, 'wk': jax.random.normal(ks[2], (D, N_KV_HEADS * HEAD_DIM), dtype=jnp.float32) * s, 'wv': jax.random.normal(ks[3], (D, N_KV_HEADS * HEAD_DIM), dtype=jnp.float32) * s, 'wo': jax.random.normal(ks[4], (D, D), dtype=jnp.float32) * s}
    _L0_attn_in = _L0_attn_setup()

    def _L0_ffn_setup():
        import jax, jax.numpy as jnp
        import numpy as np
        B, N, D = (4, 512, 256)
        SPARSITY = 0.01
        key = jax.random.key(seed)
        k1, k2, k3 = jax.random.split(key, 3)
        x = jax.random.normal(k1, (B, N, D), dtype=jnp.float32)
        spatial = jax.random.normal(k2, (D, D), dtype=jnp.float32) * 0.02
        freq = jnp.fft.fft(spatial, axis=-1)
        k = int(D * SPARSITY)
        mag = jnp.abs(freq)
        kth = jax.lax.top_k(mag, k)[0][:, -1:]
        w_sparse = jnp.where(mag >= kth, freq, 0.0 + 0j)
        bias = jax.random.normal(k3, (D,), dtype=jnp.float32) * 0.01
        return {'x': x, 'w_freq_real': jnp.real(w_sparse).astype(jnp.float32), 'w_freq_imag': jnp.imag(w_sparse).astype(jnp.float32), 'bias': bias}
    _L0_ffn_in = _L0_ffn_setup()
    _d = {'L0_attn_x': _L0_attn_in['x'], 'L0_attn_wq': _L0_attn_in['wq'], 'L0_attn_wk': _L0_attn_in['wk'], 'L0_attn_wv': _L0_attn_in['wv'], 'L0_attn_wo': _L0_attn_in['wo'], 'L0_ffn_w_freq_real': _L0_ffn_in['w_freq_real'], 'L0_ffn_w_freq_imag': _L0_ffn_in['w_freq_imag'], 'L0_ffn_bias': _L0_ffn_in['bias']}
    _x0 = _d['L0_attn_x']
    _d['L0_attn_x'] = jax.random.normal(jax.random.fold_in(jax.random.key(seed), 1), (2, 2048, 256), dtype=_x0.dtype)
    del _x0
    return _d

def reference(L0_attn_x, L0_attn_wq, L0_attn_wk, L0_attn_wv, L0_attn_wo, L0_ffn_w_freq_real, L0_ffn_w_freq_imag, L0_ffn_bias):

    def _L0_attn_ref(x, wq, wk, wv, wo):
        import jax, jax.numpy as jnp
        import numpy as np
        B, S, D = (2, 512, 256)
        N_HEADS, N_KV_HEADS = (16, 4)
        HEAD_DIM = D // N_HEADS
        KV_GROUPS = N_HEADS // N_KV_HEADS
        ROPE_BASE = 10000.0

        def _apply_rope(t, cos, sin):
            t1, t2 = jnp.split(t, 2, axis=-1)
            return jnp.concatenate([t1 * cos - t2 * sin, t1 * sin + t2 * cos], axis=-1)
        Bx, Sx, Dx = x.shape
        q = (x @ wq).reshape(Bx, Sx, N_HEADS, HEAD_DIM)
        k = (x @ wk).reshape(Bx, Sx, N_KV_HEADS, HEAD_DIM)
        v = (x @ wv).reshape(Bx, Sx, N_KV_HEADS, HEAD_DIM)
        half = HEAD_DIM // 2
        inv_freq = 1.0 / ROPE_BASE ** (jnp.arange(0, half, dtype=jnp.float32) / half)
        pos = jnp.arange(Sx, dtype=jnp.float32)
        ang = pos[:, None] * inv_freq[None, :]
        cos = jnp.cos(ang)[:, None, :]
        sin = jnp.sin(ang)[:, None, :]
        q = _apply_rope(q, cos, sin)
        k = _apply_rope(k, cos, sin)
        k = jnp.broadcast_to(k[:, :, None, :, :], (Bx, Sx, KV_GROUPS, N_KV_HEADS, HEAD_DIM)).reshape(Bx, Sx, N_HEADS, HEAD_DIM)
        v = jnp.broadcast_to(v[:, :, None, :, :], (Bx, Sx, KV_GROUPS, N_KV_HEADS, HEAD_DIM)).reshape(Bx, Sx, N_HEADS, HEAD_DIM)
        scale = 1.0 / jnp.sqrt(jnp.float32(HEAD_DIM))
        scores = jnp.einsum('bshd,bthd->bhst', q, k) * scale
        causal = jnp.tril(jnp.ones((Sx, Sx), dtype=bool))
        scores = jnp.where(causal[None, None, :, :], scores, jnp.float32(-jnp.inf))
        attn = jax.nn.softmax(scores, axis=-1)
        out = jnp.einsum('bhst,bthd->bshd', attn, v).reshape(Bx, Sx, Dx)
        return out @ wo

    def _L0_ffn_ref(x, w_freq_real, w_freq_imag, bias):
        import jax, jax.numpy as jnp
        import numpy as np
        B, N, D = (4, 512, 256)
        SPARSITY = 0.01
        w = jax.lax.complex(w_freq_real, w_freq_imag)
        x_freq = jnp.fft.fft(x, axis=-1)
        y_freq = jnp.einsum('bnd,do->bno', x_freq, w)
        y = jnp.real(jnp.fft.ifft(y_freq, axis=-1))
        return y + bias
    x = L0_attn_x
    xn = _layernorm(x, axis=-1)
    x = x + _L0_attn_ref(xn, L0_attn_wq, L0_attn_wk, L0_attn_wv, L0_attn_wo) + _L0_ffn_ref(xn, L0_ffn_w_freq_real, L0_ffn_w_freq_imag, L0_ffn_bias)
    return x

_drawn_inputs = setup_inputs


def setup_inputs(seed=0):
    import zlib

    import numpy as np

    out = dict(_drawn_inputs(seed))
    spreads = {}
    factors = {'L0_attn_wq': 8.0,
     'L0_attn_wk': 8.0,
     'L0_attn_wv': 8.0,
     'L0_attn_wo': 8.0,
     'L0_ffn_bias': 27.383}
    for name, (base, spread) in spreads.items():
        noise = np.random.default_rng([zlib.crc32(name.encode()), seed]).standard_normal(out[name].shape)
        drawn = base * np.exp(spread * noise) if base else spread * noise
        out[name] = jnp.asarray(drawn.astype(out[name].dtype))
    for name, factor in factors.items():
        out[name] = (out[name] * factor).astype(out[name].dtype)
    return out
```

```python
import concourse.bass as bass
from concourse import mybir
from contextlib import ExitStack


def attention_fourier_block(nc, x, wq, wk, wv, wo, w_re, w_im, bias, dft, rope, out):
    fp32 = mybir.dt.float32
    bf16 = mybir.dt.bfloat16
    ALU = mybir.AluOpType
    ACT = mybir.ActivationFunctionType
    AX = mybir.AxisListType

    P = 128
    NB, SEQ, D = x.shape
    KV = 4
    HD = wk.shape[1] // KV
    NH = D // HD
    R = NH // KV
    HALF = HD // 2
    TILES = SEQ // P
    CH = 512
    CT = CH // P
    NJ = SEQ // CH
    STEPS = NJ * KV
    QK = D + KV * HD
    QKV = QK + KV * HD
    KC = D // P
    PAIRS = TILES // 2
    ROWS = 3 * 2 * HD
    SHIFT = 2
    PARTS = 1024
    BLK = PARTS // P
    VW = 32
    NEG = -1.0e30
    EPS = 1e-5
    CREDIT = 2
    PAIRED = 4
    FIRST = 1
    LOADED = 16
    QUADS = KV * NJ * (NJ + 1) // 2
    OFF = QUADS - STEPS
    USES = (4, 4, 2, 2)

    x_v = x.rearrange("b (t p) d -> p (b t) d", p=P)
    out_v = out.rearrange("b (t p) d -> p (b t) d", p=P)
    scratch = nc.dram_tensor("parts_scratch", [NB * NJ, PARTS, CH], bf16, kind="Internal").ap()

    ctx = ExitStack()
    with ctx:
        def sb(name, shape, dt):
            return ctx.enter_context(nc.sbuf_tensor(name, shape, dt))

        def pb(name, shape, dt):
            return ctx.enter_context(nc.psum_tensor(name, shape, dt))

        def sem(name):
            return ctx.enter_context(nc.semaphore(name))

        x_sb = sb("x_sb", [P, NB * TILES, D], fp32)
        q_st = sb("q_st", [P, STEPS, R, CH], bf16)
        k_st = sb("k_st", [P, KV, SEQ], bf16)
        v_sb = sb("v_sb", [P, TILES, KV, VW], fp32)
        share = sb("share", [P, 12288], fp32)
        prob = share[:, 0:4096].rearrange("p (u r s) -> p u r s", u=2, r=R)
        oraw = share[:, 4096:12288].rearrange("p (n s) -> p n s", n=STEPS)
        pT = share[:, 0:4096].bitcast(bf16).rearrange("p (c k s) -> p c k s", c=2, k=BLK)
        W2 = 2 * QK
        qk_sb = share[:, 4096:4096 + 2 * W2].rearrange("p (u e n) -> p u e n", u=2, e=2)
        rc = share[:, 5376:5376 + W2].rearrange("p (e n) -> p e n", e=2)
        rs = share[:, 6016:6016 + W2].rearrange("p (e n) -> p e n", e=2)
        rot = share[:, 6656:6656 + W2].rearrange("p (e n) -> p e n", e=2)
        rest = share[:, 7296:7296 + W2].rearrange("p (e n) -> p e n", e=2)
        NT = 5
        dft_sb = share[:, 0:NT * 512].rearrange("p (m c n) -> p m c n", m=NT, c=KC)
        wf = share[:, 8192:8192 + 1024].rearrange("p (m c n) -> p m c n", m=2, c=KC)
        tT = share[:, 9216:9216 + 1024].rearrange("p (m c n) -> p m c n", m=2, c=KC)
        xn = sb("xn", [P, 2, 2, D], fp32)
        xnT = sb("xnT", [P, 2, 2, D], fp32)
        parts = sb("parts", [P, 2, 2, PARTS], bf16)
        w_sb = sb("w_sb", [P, KC, QKV + D], fp32)
        wo_sb = sb("wo_sb", [P, KC, D], fp32)
        bias_sb = sb("bias_sb", [P, D], fp32)
        rope_sb = sb("rope_sb", [P, 2, TILES, HALF], fp32)
        ident = sb("ident", [P, P], fp32)
        identb = sb("identb", [P, P], bf16)
        mask = sb("mask", [P, P], bf16)
        o_n = sb("o_n", [P, 2, D], fp32)
        o_nT = sb("o_nT", [P, 2, D], fp32)
        bn = sb("bn", [P, TILES, 6], fp32)
        stat = sb("stat", [P, TILES, 2], fp32)
        var = sb("var", [P, TILES], fp32)
        std = sb("std", [P, TILES], fp32)
        rstd = sb("rstd", [P, TILES], fp32)
        tmp = sb("tmp", [P, TILES], fp32)
        tmp2 = sb("tmp2", [P, TILES], fp32)
        pmax = sb("pmax", [P, R, CT, NJ], fp32)
        smax = sb("smax", [P, R * CT], fp32)
        mpart = sb("mpart", [R * CT, 2, P], bf16)
        rl = sb("rl", [P, NH], fp32)

        psA = pb("psA", [P, 4, 512], fp32)
        psS = pb("psS", [P, 2, 512], fp32)
        psO = pb("psO", [P, 512], fp32)
        psX = pb("psX", [P, 512], fp32)
        ps_parts = [psO[:, :].bitcast(bf16), psX[:, :].bitcast(bf16)]

        S = {n: sem(n) for n in (
            "x_in", "w_in", "table_in", "const_ready", "ones_ready", "wq_scaled", "t_acc", "t_copied", "m_acc", "m_copied",
            "bn_ready", "stat_ready", "var_ready", "std_ready", "newton", "rstd_ready",
            "xn_ready", "xn_transposed", "xnT_ready", "qkv_ready", "ffn_ready", "qk_ready", "v_ready",
            "bias_added", "base_ready", "cos_ready", "sin_ready", "rot_ready", "part1_ready", "rest_ready",
            "part2_ready", "rot_half", "parts_ready", "parts_transposed", "partsT_ready", "parts_stored", "stacks_in",
            "a_scores", "a_reduced", "smax_ready", "smax_transposed", "mhi_ready", "mpart_ready", "shift_in",
            "scores_ready", "probs_ready", "diag_masked", "pv_done", "o_copied",
            "o_transposed", "rl_ready", "o_normed", "on_transposed", "onT_ready", "wo_done", "out_ready", "out_stored", "unit_seen", "batch_seen", "sp_seen")}

        def quads_before(b, j, g):
            return b * QUADS + 2 * j * (j + 1) + g * (j + 1)

        def off_before(b, j, g):
            return b * OFF + 2 * j * (j - 1) + g * j

        def step_of(b, j, g):
            return b * STEPS + 4 * j + g

        def banks_before(b, j, g):
            return 16 * off_before(b, j, g) + sum(USES) * step_of(b, j, g)

        def target(j, half):
            return (j, 1) if half == 0 else (j + 1, 0)

        def slots(engine, b, one):
            for j in range(NJ):
                for half in range(2):
                    if (j == NJ - 1 and half == 1) or engine.engine == mybir.EngineType.PE:
                        for gi in range(2):
                            one(j, half, gi)
                    else:
                        with engine.Fori(0, 2) as gi:
                            one(j, half, gi)

        def a_plan(j, half):
            ja = target(j, half)[0]
            if ja >= NJ:
                return 0, 0, 16 * (j + 1)
            return ja + 1, 16 * (ja + 1), 16 * (j + 1)

        MT_PLACE = 8

        block = ctx.enter_context(nc.Block())

        @block.sync
        def _(sp):
            def load_x(b):
                for c in range(NJ):
                    t0 = b * TILES + c * CT
                    sp.dma_start(x_sb[:, t0:t0 + CT, :], x_v[:, t0:t0 + CT, :]).then_inc(S["x_in"], 16)

            load_x(0)
            sp.dma_start(dft_sb, dft.rearrange("m (c p) n -> p m c n", p=P)).then_inc(S["table_in"], 16)
            sp.dma_start(wf[:, 0], w_re.rearrange("(c p) n -> p c n", p=P)).then_inc(S["table_in"], 16)
            sp.dma_start(wf[:, 1], w_im.rearrange("(c p) n -> p c n", p=P)).then_inc(S["table_in"], 16)
            sp.dma_start(w_sb[:, :, 0:D], wq.rearrange("(c p) n -> p c n", p=P)).then_inc(S["w_in"], 16)
            sp.dma_start(w_sb[:, :, D:QK], wk.rearrange("(c p) n -> p c n", p=P)).then_inc(S["w_in"], 16)
            sp.dma_start(w_sb[:, :, QK:QKV], wv.rearrange("(c p) n -> p c n", p=P)).then_inc(S["w_in"], 16)
            sp.dma_start(wo_sb[:, :, :], wo.rearrange("(c p) n -> p c n", p=P)).then_inc(S["w_in"], 16)
            sp.dma_start(rope_sb[:, :, :, :], rope.rearrange("m (t p) n -> p m t n", p=P)).then_inc(S["w_in"], 16)
            sp.dma_start(bias_sb[:, :], bias.rearrange("(a n) -> a n", a=1).broadcast_to([P, D])).then_inc(S["w_in"], 16)
            sp.wait_ge(S["x_in"], 16 * NJ)
            load_x(1)
            sp.sem_inc(S["parts_stored"], CREDIT * 16)
            sp.sem_inc(S["stacks_in"], LOADED)
            sp.sem_inc(S["shift_in"], LOADED)

            with sp.Fori(0, NB) as b:
                for c in range(NJ):
                    cc = b * NJ + c
                    sp.wait_ge(S["partsT_ready"], (cc + 1) * CT + CREDIT)
                    sp.dma_start(scratch[cc].rearrange("(k p) s -> p k s", p=P), pT[:, c % 2]).then_inc(S["parts_stored"], 16)
                    sp.wait_ge(S["parts_stored"], (cc + 1 + CREDIT) * 16)
                    sp.wait_ge(S["pv_done"], b * 4 * QUADS + CREDIT)
                    sp.wait_ge(S["stacks_in"], cc * 16 * (6 * KV + 6) + LOADED)
                    for row, part in enumerate((0, 0, 1, 1, 0, 2)):
                        src = scratch[cc, part * QK:part * QK + D, :].rearrange("(r g d) s -> g d r s", r=R, g=KV)
                        for g in range(KV):
                            sp.dma_start(q_st[row * HD:(row + 1) * HD, c * KV + g, :, :], src[g]).then_inc(S["stacks_in"], 16)
                    for row, part in enumerate((0, 1, 0, 1, 2, 0)):
                        sp.dma_start(k_st[row * HD:(row + 1) * HD, :, c * CH:(c + 1) * CH],
                                     scratch[cc, part * QK + D:(part + 1) * QK, :].rearrange("(g d) s -> d g s", g=KV)).then_inc(S["stacks_in"], 16)
                sp.sem_inc(S["sp_seen"], 1)
                with sp.Fori(0, STEPS) as n:
                    sp.wait_ge(S["mpart_ready"], b * STEPS + n + 1 + FIRST)
                    for k in range(SHIFT):
                        sp.dma_start(q_st[ROWS + k:ROWS + k + 1, n, :, :].rearrange("o r (i s) -> o (r i) s", i=CT),
                                     mpart[:, k, :]).then_inc(S["shift_in"], 16)
                with sp.Fori(0, NJ) as j:
                    sp.wait_ge(S["out_ready"], b * TILES + j * CT + CT + CREDIT)
                    sp.dma_start(out_v[:, bass.ds(b * TILES + j * CT, CT), :], x_sb[:, bass.ds(b * TILES + j * CT, CT), :]).then_inc(S["out_stored"], 16)
            sp.wait_ge(S["out_stored"], NB * NJ * 16)

        @block.gpsimd
        def _(pool):
            nc.gpsimd.memset(ident[:, :], 0.0).then_inc(S["const_ready"], 1)
            nc.gpsimd.memset(identb[:, :], 0.0).then_inc(S["const_ready"], 1)
            nc.gpsimd.memset(mask[:, :], 0.0).then_inc(S["const_ready"], 1)
            nc.gpsimd.memset(v_sb[:, :, :, :], 0.0).then_inc(S["const_ready"], 1)
            nc.gpsimd.memset(parts[:, :, :, 3 * QK:PARTS], 0.0).then_inc(S["const_ready"], 1)
            pool.wait_ge(S["const_ready"], 5)
            for m in (ident, identb):
                nc.gpsimd.affine_select(out=m[:, :], in_=m[:, :], compare_op=ALU.not_equal, fill=1.0, base=0,
                                        pattern=[[-1, P]], channel_multiplier=1).then_inc(S["const_ready"], 1)
            nc.gpsimd.affine_select(out=mask[:, :], in_=mask[:, :], compare_op=ALU.is_ge, fill=NEG, base=0,
                                    pattern=[[-1, P]], channel_multiplier=1).then_inc(S["const_ready"], 1)
            nc.gpsimd.memset(v_sb[:, :, :, HD:HD + 1], 1.0).then_inc(S["const_ready"], 1)
            pool.wait_ge(S["w_in"], 96)
            with pool.Fori(0, NB) as b:
                with pool.Fori(0, PAIRS // 2) as kk:
                    for u in range(2):
                        p = b * PAIRS + kk * 2 + u
                        for e in range(2):
                            pool.wait_ge(S["xn_ready"], 2 * p + e + 1 + FIRST)
                            nc.gpsimd.tensor_tensor(x_sb[:, 2 * p + e, :], x_sb[:, 2 * p + e, :], bias_sb[:, :], ALU.add).then_inc(S["bias_added"], 1)
                        pool.wait_ge(S["qk_ready"], 2 * p + 2 + CREDIT)
                        pool.wait_ge(S["rot_ready"], p + FIRST)
                        for e in range(2):
                            cos = rope_sb[:, 0, bass.ds(kk * 4 + u * 2 + e, 1), :].rearrange("p t n -> p t n").broadcast_to([P, 2 * QK // HD, HALF])
                            nc.gpsimd.tensor_tensor(rc[:, e, :].rearrange("p (h n) -> p h n", n=HALF),
                                                    qk_sb[:, u, e, :].rearrange("p (h n) -> p h n", n=HALF), cos, ALU.mult).then_inc(S["cos_ready"], 1)
                def one(j, half, gi):
                    g = 2 * half + gi
                    n = step_of(b, j, g)
                    banks = banks_before(b, j, g) + 16 * j
                    for i in range(CT):
                        banks = banks + USES[i]
                        pool.wait_ge(S["probs_ready"], banks + CREDIT)
                        pool.sem_inc(S["unit_seen"], 1)
                        blk = prob[:, i % 2, :, i * P:(i + 1) * P]
                        nc.gpsimd.affine_select(out=blk, in_=blk, compare_op=ALU.is_ge, fill=0.0, base=0,
                                                pattern=[[0, R], [1, P]], channel_multiplier=-1).then_inc(S["diag_masked"], 1)
                slots(pool, b, one)

        @block.scalar
        def _(act):
            act.sem_inc(S["xnT_ready"], CREDIT)
            act.sem_inc(S["qk_ready"], CREDIT)
            act.sem_inc(S["v_ready"], CREDIT)
            act.sem_inc(S["partsT_ready"], CREDIT)
            act.sem_inc(S["probs_ready"], CREDIT)
            act.sem_inc(S["onT_ready"], CREDIT)
            act.sem_inc(S["o_copied"], FIRST)
            for m in range(2):
                for c in range(KC):
                    act.wait_ge(S["t_acc"], 2 * m + c + 1)
                    nc.scalar.activation(tT[:, m, c, :], psA[:, 2 * m + c, 0:D], ACT.Copy).then_inc(S["t_copied"], 1)
            act.wait_ge(S["w_in"], 96)
            for c in range(KC):
                act.wait_ge(S["m_acc"], c + 1)
                nc.scalar.activation(w_sb[:, c, QKV:QKV + D], psS[:, c, 0:D], ACT.Copy).then_inc(S["m_copied"], 1)

            with act.Fori(0, NB) as b:
                act.wait_ge(S["var_ready"], b + 1)
                nc.scalar.activation(std[:, :], var[:, :], ACT.Sqrt).then_inc(S["std_ready"], 1)

                def body(kb, u, do_x, do_qk, do_t):
                    if do_x:
                        p = b * PAIRS + kb + u
                        act.wait_ge(S["xn_transposed"], p + 1 + CREDIT)
                        act.wait_ge(S["ffn_ready"], 2 * p - 2 + PAIRED)
                        nc.scalar.activation(xnT[:, u % 2, :, :], psS[:, :, 0:D], ACT.Copy).then_inc(S["xnT_ready"], 1)
                    if do_qk:
                        p = b * PAIRS + kb + u - 1
                        par = (u - 1) % 2
                        t = kb * 2 + 2 * (u - 1)
                        act.wait_ge(S["parts_ready"], p + 1)
                        for e in range(2):
                            act.wait_ge(S["qkv_ready"], 2 * p + e + 1)
                            nc.scalar.activation(v_sb[:, t + e:t + e + 1, :, 0:HD].rearrange("p o g d -> p (o g) d"),
                                                 psA[:, 2 * e, QK:QKV].rearrange("p (g d) -> p g d", g=KV), ACT.Copy).then_inc(S["v_ready"], 1)
                            nc.scalar.activation(qk_sb[:, par, e, :], psA[:, 2 * e, 0:QK], ACT.Copy).then_inc(S["qk_ready"], 1)
                    if do_t:
                        p = b * PAIRS + kb + u - 3
                        lp = u - 3
                        ch = (lp // 2) % 2
                        act.wait_ge(S["parts_stored"], 16 * (b * NJ) + 8 * kb + 16 * (lp // 2 + 1))
                        for e in range(2):
                            act.wait_ge(S["parts_transposed"], 2 * p + e + 1 + PAIRED)
                            i = (2 * lp + e) % CT
                            nc.scalar.activation(pT[:, ch, :, i * P:(i + 1) * P],
                                                 ps_parts[e].rearrange("p (k s) -> p k s", k=BLK), ACT.Copy).then_inc(S["partsT_ready"], 1)

                for k in range(PAIRS + 3):
                    body(k - k % 4, k % 4, k < PAIRS, 1 <= k <= PAIRS, k >= 3)

                def one(j, half, gi):
                    g = 2 * half + gi
                    bank = banks_before(b, j, g)
                    unit = 4 * quads_before(b, j, g)
                    for q in range(j + 1):
                        for i in range(CT):
                            uses = USES[i] if q == j else 4
                            s0 = i * P if q == j else 0
                            hp = R // uses
                            w = CH - s0
                            act.wait_ge(S["pv_done"], unit + 1)
                            for k in range(uses):
                                act.wait_ge(S["scores_ready"], bank + 1)
                                nc.scalar.activation(prob[:, i % 2, k * hp:(k + 1) * hp, s0:CH],
                                                     psS[:, k % 2, 0:hp * w].rearrange("p (h s) -> p h s", h=hp),
                                                     ACT.Exp).then_inc(S["probs_ready"], 1)
                                bank = bank + 1
                            unit = unit + 1
                    act.wait_ge(S["pv_done"], unit + CREDIT)
                    nc.scalar.activation(oraw[:, bass.ds(4 * j + g, 1), :].rearrange("p o s -> p (o s)"), psO[:, :], ACT.Copy).then_inc(S["o_copied"], 1)
                slots(act, b, one)

                def onT(j, i):
                    t = b * TILES + 4 * j + i
                    act.wait_ge(S["on_transposed"], t + 1 + CREDIT)
                    act.wait_ge(S["wo_done"], t + 1)
                    nc.scalar.activation(o_nT[:, i % 2, :], psS[:, i % 2, 0:D], ACT.Copy).then_inc(S["onT_ready"], 1)
                with act.Fori(0, NJ) as j:
                    for i in range(CT):
                        onT(j, i)

        @block.vector
        def _(dve):
            dve.sem_inc(S["base_ready"], CREDIT)
            dve.sem_inc(S["parts_ready"], CREDIT)
            dve.sem_inc(S["a_reduced"], CREDIT)
            dve.sem_inc(S["o_normed"], CREDIT)
            dve.sem_inc(S["out_ready"], CREDIT)
            for name in ("xn_ready", "rot_ready", "rest_ready", "mpart_ready", "smax_ready"):
                dve.sem_inc(S[name], FIRST)
            nc.vector.memset(k_st[ROWS:ROWS + SHIFT, :, :], -1.0).then_inc(S["ones_ready"], 1)
            dve.wait_ge(S["w_in"], 96)
            nc.vector.tensor_scalar(w_sb[:, :, 0:D], w_sb[:, :, 0:D], float(HD) ** -0.5, None, ALU.mult).then_inc(S["wq_scaled"], 1)

            with dve.Fori(0, NB) as b:
                dve.wait_ge(S["x_in"], (b + 1) * 16 * NJ)
                dve.wait_ge(S["xn_ready"], b * TILES + FIRST)
                dve.sem_inc(S["batch_seen"], 1)
                with dve.Fori(0, TILES) as t:
                    nc.vector.bn_stats(bn[:, bass.ds(t, 1), :].rearrange("p o n -> p (o n)"),
                                       x_sb[:, bass.ds(b * TILES + t, 1), :].rearrange("p o n -> p (o n)")).then_inc(S["bn_ready"], 1)
                dve.wait_ge(S["bn_ready"], (b + 1) * TILES)
                dve.sem_inc(S["batch_seen"], 1)
                for t in range(TILES):
                    nc.vector.bn_aggr(stat[:, t, :], bn[:, t, :]).then_inc(S["stat_ready"], 1)
                dve.wait_ge(S["stat_ready"], (b + 1) * TILES)
                nc.vector.tensor_scalar(var[:, :], stat[:, :, 1], EPS, None, ALU.add).then_inc(S["var_ready"], 1)
                dve.wait_ge(S["std_ready"], b + 1)
                nc.vector.reciprocal(tmp[:, :], std[:, :]).then_inc(S["newton"], 1)
                dve.wait_ge(S["newton"], 5 * b + 1)
                nc.vector.tensor_tensor(tmp2[:, :], tmp[:, :], tmp[:, :], ALU.mult).then_inc(S["newton"], 1)
                dve.wait_ge(S["newton"], 5 * b + 2)
                nc.vector.tensor_tensor(std[:, :], tmp2[:, :], var[:, :], ALU.mult).then_inc(S["newton"], 1)
                dve.wait_ge(S["newton"], 5 * b + 3)
                nc.vector.tensor_scalar(tmp2[:, :], std[:, :], -0.5, 1.5, ALU.mult, ALU.add).then_inc(S["newton"], 1)
                dve.wait_ge(S["newton"], 5 * b + 4)
                nc.vector.tensor_tensor(rstd[:, :], tmp[:, :], tmp2[:, :], ALU.mult).then_inc(S["newton"], 1)
                dve.wait_ge(S["newton"], 5 * b + 5)

                def body(kb, u, do_n, do_r):
                    if do_n:
                        p = b * PAIRS + kb + u
                        dve.wait_ge(S["xn_transposed"], p + 1)
                        for e in range(2):
                            t = kb * 2 + 2 * u + e
                            nc.vector.tensor_scalar(xn[:, u % 2, e, :], x_sb[:, bass.ds(b * TILES + t, 1), :].rearrange("p o n -> p (o n)"),
                                                    stat[:, bass.ds(t, 1), 0:1].rearrange("p o n -> p (o n)"), rstd[:, bass.ds(t, 1)],
                                                    ALU.subtract, ALU.mult).then_inc(S["xn_ready"], 1)
                    if do_r:
                        p = b * PAIRS + kb + u - 2
                        par = u % 2
                        src = qk_sb[:, par].rearrange("p e (h m n) -> p e h m n", m=2, n=HALF)
                        dst = rs.rearrange("p e (h m n) -> p e h m n", m=2, n=HALF)
                        dve.wait_ge(S["qk_ready"], 2 * p + 2 + CREDIT)
                        dve.wait_ge(S["rot_ready"], p + FIRST)
                        for e in range(2):
                            sin = rope_sb[:, 1, bass.ds(kb * 2 + 2 * (u - 2) + e, 1), :].broadcast_to([P, QK // HD, HALF])
                            nc.vector.tensor_tensor(dst[:, e, :, 0, :], src[:, e, :, 1, :], sin, ALU.mult).then_inc(S["sin_ready"], 1)
                            nc.vector.tensor_tensor(dst[:, e, :, 1, :], src[:, e, :, 0, :], sin, ALU.mult).then_inc(S["sin_ready"], 1)
                        dve.wait_ge(S["sin_ready"], 4 * p + 4)
                        dve.wait_ge(S["cos_ready"], 2 * p + 2)
                        dve.wait_ge(S["rest_ready"], p + FIRST)
                        rot_v = rot.rearrange("p e (h m n) -> p (e h) m n", m=2, n=HALF)
                        rc_v = rc.rearrange("p e (h m n) -> p (e h) m n", m=2, n=HALF)
                        rs_v = rs.rearrange("p e (h m n) -> p (e h) m n", m=2, n=HALF)
                        nc.vector.tensor_tensor(rot_v[:, :, 0, :], rc_v[:, :, 0, :], rs_v[:, :, 0, :], ALU.subtract).then_inc(S["rot_half"], 1)
                        nc.vector.tensor_tensor(rot_v[:, :, 1, :], rc_v[:, :, 1, :], rs_v[:, :, 1, :], ALU.add).then_inc(S["rot_ready"], 1)
                        dve.wait_ge(S["rot_half"], p + 1)
                        dve.wait_ge(S["rot_ready"], p + 1 + FIRST)
                        dve.wait_ge(S["parts_transposed"], 2 * p - 2 + PAIRED)
                        part = [parts[:, par, :, k * QK:(k + 1) * QK] for k in range(3)]
                        nc.vector.tensor_copy(part[0], rot).then_inc(S["part1_ready"], 1)
                        dve.wait_ge(S["part1_ready"], p + 1)
                        dve.wait_ge(S["parts_ready"], p + CREDIT)
                        nc.vector.tensor_tensor(rest, rot, part[0], ALU.subtract).then_inc(S["rest_ready"], 1)
                        dve.wait_ge(S["rest_ready"], p + 1 + FIRST)
                        nc.vector.tensor_copy(part[1], rest).then_inc(S["part2_ready"], 1)
                        dve.wait_ge(S["part2_ready"], p + 1)
                        nc.vector.tensor_tensor(part[2], rest, part[1], ALU.subtract).then_inc(S["parts_ready"], 1)
                        for e in range(2):
                            dve.wait_ge(S["ffn_ready"], 2 * p + e + 1 + PAIRED)
                            dve.wait_ge(S["bias_added"], 2 * p + e + 1)
                            xt = x_sb[:, bass.ds(2 * p + e, 1), :].rearrange("p o n -> p (o n)")
                            nc.vector.tensor_tensor(xt, psA[:, 2 * e + 1, 0:D], xt, ALU.add).then_inc(S["base_ready"], 1)

                for u in range(2):
                    body(0, u, True, False)
                with dve.Fori(0, (PAIRS - 2) // 2) as kk:
                    for u in range(2):
                        body(kk * 2, u + 2, True, True)
                for u in range(2):
                    body(PAIRS, u, False, True)

                def reduce(m, nq, v0):
                    q, i, h2 = m // 8, (m % 8) // 2, m % 2
                    w = (i + 1) * P if q == nq - 1 else CH
                    dve.wait_ge(S["a_scores"], v0 + m + 1)
                    nc.vector.reduce_max(pmax[:, 2 * h2:2 * h2 + 2, i, q], psA[:, 2 * h2:2 * h2 + 2, 0:w], AX.X).then_inc(S["a_reduced"], 1)

                def combine(nq, v0, n):
                    dve.wait_ge(S["a_reduced"], v0 + 8 * nq + CREDIT)
                    dve.wait_ge(S["smax_transposed"], n + FIRST)
                    nc.vector.reduce_max(smax[:, :], pmax[:, :, :, 0:nq].rearrange("p r i q -> p (r i) q"), AX.X).then_inc(S["smax_ready"], 1)

                def shift(n):
                    dve.wait_ge(S["smax_transposed"], n + 1 + FIRST)
                    dve.wait_ge(S["shift_in"], n * 16 * SHIFT + LOADED)
                    nc.vector.tensor_copy(mpart[:, 0, :], psX[0:R * CT, 0:P]).then_inc(S["mhi_ready"], 1)
                    dve.wait_ge(S["mhi_ready"], n + 1)
                    nc.vector.tensor_tensor(mpart[:, 1, :], psX[0:R * CT, 0:P], mpart[:, 0, :], ALU.subtract).then_inc(S["mpart_ready"], 1)

                for g in range(2):
                    v0 = 8 * quads_before(b, 0, g)
                    dve.wait_ge(S["smax_ready"], step_of(b, 0, g) + FIRST)
                    for m in range(8):
                        reduce(m, 1, v0)
                    if g == 1:
                        shift(step_of(b, 0, 0))
                    combine(1, v0, step_of(b, 0, g))

                def one(j, half, gi):
                    g = 2 * half + gi
                    n = step_of(b, j, g)
                    nq, mm, places = a_plan(j, half)
                    last = isinstance(gi, int) and j == NJ - 1 and half == 1 and gi == 1
                    if nq:
                        ja = nq - 1
                        ga = (2 if half == 0 else 0) + gi
                        v0 = 8 * quads_before(b, ja, ga)
                        dve.wait_ge(S["smax_ready"], n + 2 + FIRST)
                    before = (MT_PLACE * mm // places) // 2
                    for m in range(before):
                        reduce(m, nq, v0)
                    if not last:
                        shift(n + 1)
                    if nq:
                        for m in range(before, mm // 2):
                            reduce(m, nq, v0)
                        combine(nq, v0, n + 2)
                slots(dve, b, one)

                def norm(j, i):
                    t = b * TILES + 4 * j + i
                    dve.wait_ge(S["o_transposed"], t + 1)
                    o = psA[:, i % 2, :].rearrange("p (g r w) -> p g r w", g=KV, r=R)
                    dve.wait_ge(S["o_normed"], t + CREDIT)
                    nc.vector.reciprocal(rl[:, :].rearrange("p (g r o) -> p g r o", g=KV, o=1), o[:, :, :, HD:HD + 1]).then_inc(S["rl_ready"], 1)
                    dve.wait_ge(S["rl_ready"], t + 1)
                    dve.wait_ge(S["on_transposed"], t + 1)
                    nc.vector.tensor_tensor(o_n[:, i % 2, :].rearrange("p (r g d) -> p g r d", r=R, g=KV), o[:, :, :, 0:HD],
                                            rl[:, :].rearrange("p (g r o) -> p g r o", g=KV, o=1).broadcast_to([P, KV, R, HD]),
                                            ALU.mult).then_inc(S["o_normed"], 1)

                def add(j, i):
                    t = b * TILES + 4 * j + i
                    dve.wait_ge(S["wo_done"], t + 1 + CREDIT)
                    xt = x_sb[:, bass.ds(t, 1), :].rearrange("p o n -> p (o n)")
                    nc.vector.tensor_tensor(xt, psA[:, 2 + i % 2, 0:D], xt, ALU.add).then_inc(S["out_ready"], 1)

                for i in range(CT):
                    norm(0, i)
                    if i >= 2:
                        add(0, i - 2)
                with dve.Fori(1, NJ) as j:
                    for i in range(CT):
                        norm(j, i)
                        if i >= 2:
                            add(j, i - 2)
                        else:
                            add(j - 1, i + 2)
                for i in (2, 3):
                    add(NJ - 1, i)

        @block.tensor
        def _(pe):
            mm = nc.tensor.matmul
            pe.sem_inc(S["xn_transposed"], CREDIT)
            pe.sem_inc(S["ffn_ready"], PAIRED)
            pe.sem_inc(S["parts_transposed"], PAIRED)
            pe.sem_inc(S["smax_transposed"], FIRST)
            pe.sem_inc(S["pv_done"], CREDIT)
            pe.sem_inc(S["on_transposed"], CREDIT)
            pe.sem_inc(S["wo_done"], CREDIT)
            pe.wait_ge(S["table_in"], 48)
            C, SN, NSN, CN, NSNN = range(NT)
            for m, terms in enumerate((((0, C), (1, SN)), ((1, C), (0, NSN)))):
                for c in range(KC):
                    for k, (w, f) in enumerate(terms):
                        for d in range(KC):
                            last = mm(psA[:, 2 * m + c, 0:D], wf[:, w, d, c * P:(c + 1) * P], dft_sb[:, f, d, :],
                                      start=(k == 0 and d == 0), stop=(k == 1 and d == KC - 1))
                    last.then_inc(S["t_acc"], 1)
            pe.wait_ge(S["t_copied"], 4)
            for c in range(KC):
                for m, f in enumerate((CN, NSNN)):
                    for d in range(KC):
                        last = mm(psS[:, c, 0:D], tT[:, m, d, c * P:(c + 1) * P], dft_sb[:, f, d, :],
                                  start=(m == 0 and d == 0), stop=(m == 1 and d == KC - 1))
                last.then_inc(S["m_acc"], 1)
            pe.wait_ge(S["m_copied"], 2)
            pe.wait_ge(S["const_ready"], 9)
            pe.wait_ge(S["ones_ready"], 1)
            pe.wait_ge(S["wq_scaled"], 1)

            with pe.Fori(0, NB) as b:
                pe.wait_ge(S["out_ready"], b * TILES + CREDIT)

                def body(kb, u, do_x, do_qkv, do_t):
                    if do_x:
                        p = b * PAIRS + kb + u
                        pe.wait_ge(S["xn_ready"], 2 * p + 2 + FIRST)
                        pe.wait_ge(S["xnT_ready"], p + CREDIT)
                        for e in range(2):
                            for c in range(KC):
                                last = nc.tensor.transpose(psS[:, e, c * P:(c + 1) * P], xn[:, u % 2, e, c * P:(c + 1) * P], ident[:, :])
                        last.then_inc(S["xn_transposed"], 1)
                    if do_qkv:
                        p = b * PAIRS + kb + u - 1
                        par = (u - 1) % 2
                        pe.wait_ge(S["xnT_ready"], p + 1 + CREDIT)
                        for e in range(2):
                            pe.wait_ge(S["qk_ready"], 2 * p + e + 1)
                            pe.wait_ge(S["v_ready"], 2 * p + e + 1)
                            for c in range(KC):
                                last = mm(psA[:, 2 * e, 0:QKV], xnT[:, par, e, c * P:(c + 1) * P], w_sb[:, c, 0:QKV], start=(c == 0), stop=(c == KC - 1))
                            last.then_inc(S["qkv_ready"], 1)
                            pe.wait_ge(S["base_ready"], 2 * p + e + 1)
                            for c in range(KC):
                                last = mm(psA[:, 2 * e + 1, 0:D], xnT[:, par, e, c * P:(c + 1) * P], w_sb[:, c, QKV:QKV + D], start=(c == 0), stop=(c == KC - 1))
                            last.then_inc(S["ffn_ready"], 1)
                    if do_t:
                        p = b * PAIRS + kb + u - 3
                        par = (u - 3) % 2
                        pe.wait_ge(S["parts_ready"], p + 1 + CREDIT)
                        for e in range(2):
                            pe.wait_ge(S["partsT_ready"], 2 * p + e + 1)
                            for k in range(BLK):
                                last = nc.tensor.transpose(ps_parts[e][:, k * P:(k + 1) * P], parts[:, par, e, k * P:(k + 1) * P], identb[:, :])
                            last.then_inc(S["parts_transposed"], 1)

                for k in range(PAIRS + 3):
                    body(k - k % 4, k % 4, k < PAIRS, 1 <= k <= PAIRS, k >= 3)
                pe.wait_ge(S["partsT_ready"], (b + 1) * TILES + CREDIT)
                pe.wait_ge(S["base_ready"], (b + 1) * TILES + CREDIT)
                pe.wait_ge(S["v_ready"], (b + 1) * TILES + CREDIT)
                pe.wait_ge(S["qk_ready"], (b + 1) * TILES + CREDIT)

                def a_scores(h, nq, na, ga, v0):
                    m, h1 = h // 2, h % 2
                    q, i, h2 = m // 8, (m % 8) // 2, m % 2
                    r = 2 * h2 + h1
                    diag = q == nq - 1
                    w = (i + 1) * P if diag else CH
                    if h1 == 0:
                        pe.wait_ge(S["a_reduced"], v0 + m + 1)
                    last = mm(psA[:, r, 0:w], q_st[0:ROWS, na, r, i * P:(i + 1) * P], k_st[0:ROWS, ga, q * CH:q * CH + w], start=True, stop=not diag)
                    if diag:
                        last = mm(psA[:, r, w - P:w], identb[:, :], mask[:, :], start=False, stop=True)
                    if h1 == 1:
                        last.then_inc(S["a_scores"], 1)

                def transpose_max(n):
                    pe.wait_ge(S["smax_ready"], n + 1 + FIRST)
                    pe.wait_ge(S["mpart_ready"], n + FIRST)
                    nc.tensor.transpose(psX[0:R * CT, 0:P], smax[:, :], ident[:, :]).then_inc(S["smax_transposed"], 1)

                loads = 16 * (6 * KV + 6)
                pe.wait_ge(S["stacks_in"], (b * NJ + 1) * loads + LOADED)
                for g in range(2):
                    for h in range(16):
                        a_scores(h, 1, g, g, 8 * quads_before(b, 0, g))
                    if g == 0:
                        transpose_max(step_of(b, 0, 0))

                def one(j, half, gi):
                    g = 2 * half + gi
                    n = step_of(b, j, g)
                    nl = 4 * j + g
                    nq, total, places = a_plan(j, half)
                    last_step = j == NJ - 1 and half == 1 and gi == 1
                    if nq:
                        ja = nq - 1
                        ga = (2 if half == 0 else 0) + gi
                        v0 = 8 * quads_before(b, ja, ga)
                        pe.wait_ge(S["stacks_in"], (b * NJ + ja + 1) * loads + LOADED)
                    bank = banks_before(b, j, g)
                    unit = 4 * quads_before(b, j, g)
                    pe.wait_ge(S["shift_in"], (n + 1) * 16 * SHIFT + LOADED)

                    def pv(u, ready):
                        q, i = u // CT, u % CT
                        s0 = i * P if q == j else 0
                        if u == 0:
                            pe.wait_ge(S["o_copied"], n + FIRST)
                        if q == j:
                            pe.wait_ge(S["diag_masked"], 4 * n + i + 1)
                        else:
                            pe.wait_ge(S["probs_ready"], ready + CREDIT)
                        for r in range(R):
                            last = mm(psO[32 * r:32 * r + VW, s0:CH], v_sb[:, u, g, :], prob[:, i % 2, r, s0:CH],
                                      start=(u == 0), stop=(u == 4 * j + 3), tile_position=(0, 32 * r))
                        last.then_inc(S["pv_done"], 1)

                    place = 0
                    done = 0
                    for u in range(4 * (j + 1)):
                        q, i = u // CT, u % CT
                        uses = USES[i] if q == j else 4
                        s0 = i * P if q == j else 0
                        hp = R // uses
                        w = CH - s0
                        ready = bank
                        for r in range(R):
                            if r % hp == 0:
                                pe.wait_ge(S["probs_ready"], bank + 1)
                            o = (r % hp) * w
                            last = mm(psS[:, (r // hp) % 2, o:o + w], k_st[0:ROWS + SHIFT, g, u * P:(u + 1) * P],
                                      q_st[0:ROWS + SHIFT, nl, r, s0:CH], start=True, stop=True)
                            if r % hp == hp - 1:
                                last.then_inc(S["scores_ready"], 1)
                                bank = bank + 1
                            place += 1
                            while done < place * total // places:
                                a_scores(done, nq, nl + 2, ga, v0)
                                done += 1
                            if r == 1 and u > 0:
                                pv(u - 1, ready)
                        if place == MT_PLACE and not last_step:
                            transpose_max(n + 1)
                    pv(4 * j + 3, bank)

                slots(pe, b, one)

                pe.wait_ge(S["o_copied"], (b + 1) * STEPS + FIRST)
                pe.wait_ge(S["a_reduced"], (b + 1) * 8 * QUADS + CREDIT)

                def tr_o(j, i):
                    t = b * TILES + 4 * j + i
                    pe.wait_ge(S["o_normed"], t + 1)
                    for g in range(KV):
                        last = nc.tensor.transpose(psA[:, i % 2, g * P:(g + 1) * P],
                                                   oraw[:, 4 * j + g, i * P:(i + 1) * P], ident[:, :])
                    last.then_inc(S["o_transposed"], 1)

                def tr_n(j, i):
                    t = b * TILES + 4 * j + i
                    pe.wait_ge(S["o_normed"], t + 1 + CREDIT)
                    pe.wait_ge(S["onT_ready"], t + 1)
                    for c in range(KC):
                        last = nc.tensor.transpose(psS[:, i % 2, c * P:(c + 1) * P], o_n[:, i % 2, c * P:(c + 1) * P], ident[:, :])
                    last.then_inc(S["on_transposed"], 1)

                def project(j, i):
                    t = b * TILES + 4 * j + i
                    pe.wait_ge(S["onT_ready"], t + 1 + CREDIT)
                    pe.wait_ge(S["out_ready"], t + 1)
                    for c in range(KC):
                        last = mm(psA[:, 2 + i % 2, 0:D], o_nT[:, i % 2, c * P:(c + 1) * P], wo_sb[:, c, :], start=(c == 0), stop=(c == KC - 1))
                    last.then_inc(S["wo_done"], 1)

                for t in range(TILES + 2):
                    if t < TILES:
                        tr_o(t // CT, t % CT)
                    if 1 <= t <= TILES:
                        tr_n((t - 1) // CT, (t - 1) % CT)
                    if t >= 2:
                        project((t - 2) // CT, (t - 2) % CT)


_INS = ["L0_attn_x", "L0_attn_wq", "L0_attn_wk", "L0_attn_wv", "L0_attn_wo",
        "L0_ffn_w_freq_real", "L0_ffn_w_freq_imag", "L0_ffn_bias"]


def kernel(**inputs):
    import numpy as _np
    import concourse.bacc as _bacc
    from concourse import mybir as _mybir
    from concourse.bass_utils import run_bass_kernel_spmd as _run

    nc = _bacc.Bacc("TRN2", target_bir_lowering=False, num_devices=1)
    arrays, args = {}, []

    def give(name, a):
        arrays[name] = a
        args.append(nc.dram_tensor(name, a.shape, _mybir.dt.from_np(a.dtype), kind="ExternalInput").ap())

    for name in _INS:
        give(f"in_{name}", _np.ascontiguousarray(inputs[name]))
    N = 256
    turn = 2.0 * _np.pi * ((_np.arange(N)[:, None] * _np.arange(N)[None, :]) % N) / N
    c, s = _np.cos(turn), _np.sin(turn)
    give("dft_tables", _np.stack([c, s, -s, c / N, -s / N]).astype(_np.float32))
    inv = (1.0 / _np.float32(10000.0) ** (_np.arange(8, dtype=_np.float32) / _np.float32(8))).astype(_np.float32)
    ang = (_np.arange(2048, dtype=_np.float32)[:, None] * inv[None, :]).astype(_np.float32)
    give("rope_tables", _np.stack([_np.cos(ang), _np.sin(ang)]).astype(_np.float32))
    out = nc.dram_tensor("out_0", (2, 2048, 256), _mybir.dt.float32, kind="ExternalOutput").ap()
    attention_fourier_block(nc, *args, out)
    r = _run(nc, [arrays], core_ids=[0])
    return r.results[0]["out_0"]
```

```python
import concourse.bass as bass
from concourse import mybir
from contextlib import ExitStack


def attention_fourier_block(nc, x, wq, wk, wv, wo, w_re, w_im, bias, dft, rope, out):
    fp32 = mybir.dt.float32
    bf16 = mybir.dt.bfloat16
    ALU = mybir.AluOpType
    ACT = mybir.ActivationFunctionType
    AX = mybir.AxisListType

    P = 128
    NB, SEQ, D = x.shape
    KV = 4
    HD = wk.shape[1] // KV
    NH = D // HD
    R = NH // KV
    HALF = HD // 2
    TILES = SEQ // P
    CH = 512
    CT = CH // P
    NJ = SEQ // CH
    STEPS = NJ * KV
    QK = D + KV * HD
    QKV = QK + KV * HD
    KC = D // P
    PAIRS = TILES // 2
    ROWS = 3 * 2 * HD
    SHIFT = 2
    PARTS = 1024
    BLK = PARTS // P
    VW = 32
    LOADS = 12
    NEG = -1.0e30
    EPS = 1e-5
    CREDIT = 2
    PAIRED = 4
    FIRST = 1
    LOADED = 16
    QUADS = KV * NJ * (NJ + 1) // 2
    OFF = QUADS - STEPS
    USES = (4, 4, 2, 2)

    x_v = x.rearrange("b (t p) d -> p (b t) d", p=P)
    out_v = out.rearrange("b (t p) d -> p (b t) d", p=P)
    scratch = nc.dram_tensor("parts_scratch", [NB * NJ, PARTS, CH], bf16, kind="Internal").ap()

    ctx = ExitStack()
    with ctx:
        def sb(name, shape, dt):
            return ctx.enter_context(nc.sbuf_tensor(name, shape, dt))

        def pb(name, shape, dt):
            return ctx.enter_context(nc.psum_tensor(name, shape, dt))

        def sem(name):
            return ctx.enter_context(nc.semaphore(name))

        x_sb = sb("x_sb", [P, NB * TILES, D], fp32)
        q_st = sb("q_st", [P, STEPS, R, CH], bf16)
        k_st = sb("k_st", [P, KV, SEQ], bf16)
        v_sb = sb("v_sb", [P, TILES, KV, VW], fp32)
        share = sb("share", [P, 12288], fp32)
        prob = share[:, 0:4096].rearrange("p (u r s) -> p u r s", u=2, r=R)
        oraw = share[:, 4096:12288].rearrange("p (n s) -> p n s", n=STEPS)
        pT = share[:, 0:4096].bitcast(bf16).rearrange("p (c k s) -> p c k s", c=2, k=BLK)
        W2 = 2 * QK
        qk_sb = share[:, 4096:4096 + 2 * W2].rearrange("p (u e n) -> p u e n", u=2, e=2)
        rc = share[:, 5376:5376 + W2].rearrange("p (e n) -> p e n", e=2)
        rs = share[:, 6016:6016 + W2].rearrange("p (e n) -> p e n", e=2)
        rot = share[:, 6656:6656 + W2].rearrange("p (e n) -> p e n", e=2)
        rest = share[:, 7296:7296 + W2].rearrange("p (e n) -> p e n", e=2)
        ffn_sb = share[:, 7936:7936 + 4 * D].rearrange("p (u e n) -> p u e n", u=2, e=2)
        NT = 2
        dft_sb = share[:, 0:NT * 512].rearrange("p (m c n) -> p m c n", m=NT, c=KC)
        wf = share[:, 4096:4096 + 1536].rearrange("p (m c n) -> p m c n", m=3, c=KC)
        wq_raw = share[:, 5632:6144].rearrange("p (c n) -> p c n", c=KC)
        tT = share[:, 9216:9216 + 1024].rearrange("p (m c n) -> p m c n", m=2, c=KC)
        xn = sb("xn", [P, 2, 2, D], fp32)
        xnT = sb("xnT", [P, 2, 2, D], fp32)
        parts = sb("parts", [P, 2, 2, PARTS], bf16)
        w_sb = sb("w_sb", [P, KC, QKV + D], fp32)
        wo_sb = sb("wo_sb", [P, KC, D], fp32)
        bias_sb = sb("bias_sb", [P, D], fp32)
        bias_r = sb("bias_r", [P, D], fp32)
        bias_c = sb("bias_c", [P, 3, D], bf16)
        bias_p = sb("bias_p", [P, D], bf16)
        ones = sb("ones", [P, P], bf16)
        rope_sb = sb("rope_sb", [P, 2, TILES, HALF], fp32)
        ident = sb("ident", [P, P], fp32)
        identb = sb("identb", [P, P], bf16)
        mask = sb("mask", [P, P], bf16)
        o_n = sb("o_n", [P, 2, D], fp32)
        o_nT = sb("o_nT", [P, 2, D], fp32)
        bn = sb("bn", [P, NB * TILES, 6], fp32)
        stat = sb("stat", [P, NB * TILES, 2], fp32)
        var = sb("var", [P, NB * TILES], fp32)
        std = sb("std", [P, NB * TILES], fp32)
        rstd = sb("rstd", [P, NB * TILES], fp32)
        tmp = sb("tmp", [P, NB * TILES], fp32)
        tmp2 = sb("tmp2", [P, NB * TILES], fp32)
        pmax = sb("pmax", [P, R, CT, NJ], fp32)
        smax = sb("smax", [P, R * CT], fp32)
        mpart = sb("mpart", [R * CT, 2, P], bf16)
        rl = sb("rl", [P, NH], fp32)

        psA = pb("psA", [P, 4, 512], fp32)
        psS = pb("psS", [P, 2, 512], fp32)
        psO = pb("psO", [P, 512], fp32)
        psX = pb("psX", [P, 512], fp32)
        ps_parts = [psO[:, :].bitcast(bf16), psX[:, :].bitcast(bf16)]

        S = {n: sem(n) for n in (
            "w_in", "table_in", "const_ready", "ones_ready", "negated", "wq_scaled", "t_acc", "t_copied", "m_acc", "m_copied",
            "bn_ready", "stat_ready", "var_ready", "std_ready", "newton", "rstd_ready",
            "xn_ready", "xn_transposed", "xnT_ready", "qkv_ready", "ffn_ready", "qk_ready", "v_ready",
            "ffn_copied", "base_ready", "bias_step", "bias_ready", "cos_ready", "sin_ready", "rot_ready", "part1_ready", "rest_ready",
            "part2_ready", "rot_half", "parts_ready", "parts_transposed", "partsT_ready", "parts_stored", "stacks_in",
            "a_scores", "a_reduced", "smax_ready", "smax_transposed", "mhi_ready", "mpart_ready", "shift_in",
            "scores_ready", "probs_ready", "diag_masked", "pv_done", "o_copied",
            "o_transposed", "rl_ready", "o_normed", "on_transposed", "onT_ready", "wo_done", "out_ready", "out_stored", "unit_seen", "batch_seen", "sp_seen")}

        x_in = [sem(f"x_in{c}") for c in range(NJ)]

        def quads_before(b, j, g):
            return b * QUADS + 2 * j * (j + 1) + g * (j + 1)

        def off_before(b, j, g):
            return b * OFF + 2 * j * (j - 1) + g * j

        def step_of(b, j, g):
            return b * STEPS + 4 * j + g

        def n_in_batch(j, g):
            return 4 * j + g

        def banks_before(b, j, g):
            return 16 * off_before(b, j, g) + sum(USES) * step_of(b, j, g)

        def slots(engine, b, one):
            for j in range(NJ):
                low = 1 if j == 0 else 0
                high = KV - 1 if j == NJ - 1 else KV
                if low:
                    one(j, 0)
                with engine.Fori(low, high) as g:
                    one(j, g)
                if high < KV:
                    one(j, KV - 1)

        def a_use(v):
            n = 0
            while v >= 8 * (n // KV + 1):
                v -= 8 * (n // KV + 1)
                n += 1
            return n, n // KV + 1, v

        PRE = 16
        ALL = 8 * QUADS
        SLACK = 2.0

        def a_weight(v):
            n, nq, m = a_use(v)
            return 1.0 if m < 8 * (nq - 1) else 0.1 + 0.9 * ((m % 8) // 2 + 1) / CT

        def b_weight(n, u):
            return 1.0 if u < 4 * (n // KV) else 0.1 + 0.9 * (1 - (u % CT) / CT)

        dates = []
        begins, total = 0.0, 0.0
        for n in range(STEPS):
            nq = n // KV + 1
            total += sum(a_weight(v) for v in range(ALL) if a_use(v)[0] == n)
            if n > 1:
                dates.append((begins - SLACK, total))
            begins += sum(b_weight(n, u) for u in range(4 * nq))
        plan, turn = [], []
        at, done, aim, spent, turned = PRE, sum(a_weight(v) for v in range(PRE)), None, 0.0, 1
        aim = done
        for n in range(STEPS):
            plan.append([])
            turn.append([])
            for u in range(4 * (n // KV + 1)):
                w = b_weight(n, u)
                rate = max([(need - aim) / max(date - spent, w) for date, need in dates if need > aim + 1e-9], default=0.0)
                aim += rate * w
                spent += w
                before = at
                while at < ALL and done + a_weight(at) <= aim + 0.01:
                    done += a_weight(at)
                    at += 1
                plan[-1].append(at)
                ripe = 2 if n == 0 and u == 0 else (a_use(before)[0] if before < ALL else STEPS)
                turns = min(ripe, turned + 1)
                turn[-1].append(turned if turned < turns else None)
                turned = turns
        assert at == ALL and turned == STEPS
        for n in range(STEPS - 1):
            flat = [x for row in turn[:n + 1] for x in row]
            assert n + 1 in flat or n + 1 == 0

        def score_bank(tail, uses, i, k):
            if tail and (k >= 2 or (uses == 2 and i == CT - 1)):
                return psA[:, k % 2, :]
            return psS[:, k % 2, :]

        block = ctx.enter_context(nc.Block())

        @block.sync
        def _(sp):
            def load_x(b):
                for c in range(NJ):
                    t0 = b * TILES + c * CT
                    sp.dma_start(x_sb[:, t0:t0 + CT, :], x_v[:, t0:t0 + CT, :]).then_inc(x_in[c], 16)

            def load_shift(b, n):
                sp.wait_ge(S["mpart_ready"], b * STEPS + n + 1 + FIRST)
                for k in range(SHIFT):
                    sp.dma_start(q_st[ROWS + k:ROWS + k + 1, n, :, :].rearrange("o r (i s) -> o (r i) s", i=CT),
                                 mpart[:, k, :]).then_inc(S["shift_in"], 16)

            load_x(0)
            sp.dma_start(dft_sb, dft.rearrange("m (c p) n -> p m c n", p=P)).then_inc(S["table_in"], 16)
            sp.dma_start(wf[:, 0], w_re.rearrange("(c p) n -> p c n", p=P)).then_inc(S["table_in"], 16)
            sp.dma_start(wf[:, 1], w_im.rearrange("(c p) n -> p c n", p=P)).then_inc(S["table_in"], 16)
            sp.dma_start(wq_raw, wq.rearrange("(c p) n -> p c n", p=P)).then_inc(S["w_in"], 16)
            sp.dma_start(w_sb[:, :, D:QK], wk.rearrange("(c p) n -> p c n", p=P)).then_inc(S["w_in"], 16)
            sp.dma_start(w_sb[:, :, QK:QKV], wv.rearrange("(c p) n -> p c n", p=P)).then_inc(S["w_in"], 16)
            sp.dma_start(wo_sb[:, :, :], wo.rearrange("(c p) n -> p c n", p=P)).then_inc(S["w_in"], 16)
            sp.dma_start(rope_sb[:, :, :, :], rope.rearrange("m (t p) n -> p m t n", p=P)).then_inc(S["w_in"], 16)
            sp.dma_start(bias_sb[:, :], bias.rearrange("(a n) -> a n", a=1).broadcast_to([P, D])).then_inc(S["w_in"], 16)
            for c in range(NJ):
                sp.wait_ge(x_in[c], 16)
            load_x(1)
            sp.sem_inc(S["parts_stored"], CREDIT * 16)
            sp.sem_inc(S["stacks_in"], LOADED)
            sp.sem_inc(S["shift_in"], LOADED)

            with sp.Fori(0, NB) as b:
                for c in range(NJ):
                    cc = b * NJ + c
                    sp.wait_ge(S["partsT_ready"], (cc + 1) * CT + CREDIT)
                    sp.dma_start(scratch[cc].rearrange("(k p) s -> p k s", p=P), pT[:, c % 2]).then_inc(S["parts_stored"], 16)
                    if c == NJ - 1:
                        load_shift(b, 0)
                    sp.wait_ge(S["parts_stored"], (cc + 1 + CREDIT) * 16)
                    sp.wait_ge(S["pv_done"], b * 4 * QUADS + CREDIT)
                    sp.wait_ge(S["stacks_in"], cc * 16 * LOADS + LOADED)
                    for row, part in enumerate((0, 0, 1, 1, 0, 2)):
                        sp.dma_start(q_st[row * HD:(row + 1) * HD, c * KV:(c + 1) * KV, :, :].rearrange("d g r s -> d (g r) s"),
                                     scratch[cc, part * QK:part * QK + D, :].rearrange("(h d) s -> d h s", h=NH)).then_inc(S["stacks_in"], 16)
                    for row, part in enumerate((0, 1, 0, 1, 2, 0)):
                        sp.dma_start(k_st[row * HD:(row + 1) * HD, :, c * CH:(c + 1) * CH],
                                     scratch[cc, part * QK + D:(part + 1) * QK, :].rearrange("(g d) s -> d g s", g=KV)).then_inc(S["stacks_in"], 16)
                with sp.Fori(1, STEPS) as n:
                    load_shift(b, n)
                with sp.Fori(0, NJ) as j:
                    sp.wait_ge(S["out_ready"], b * TILES + j * CT + CT + CREDIT)
                    sp.dma_start(out_v[:, bass.ds(b * TILES + j * CT, CT), :], x_sb[:, bass.ds(b * TILES + j * CT, CT), :]).then_inc(S["out_stored"], 16)
            sp.wait_ge(S["out_stored"], NB * NJ * 16)

        @block.gpsimd
        def _(pool):
            nc.gpsimd.memset(ident[:, :], 0.0).then_inc(S["const_ready"], 1)
            nc.gpsimd.memset(identb[:, :], 0.0).then_inc(S["const_ready"], 1)
            nc.gpsimd.memset(mask[:, :], 0.0).then_inc(S["const_ready"], 1)
            nc.gpsimd.memset(v_sb[:, :, :, :], 0.0).then_inc(S["const_ready"], 1)
            nc.gpsimd.memset(ones[:, :], 1.0).then_inc(S["const_ready"], 1)
            nc.gpsimd.memset(parts[:, :, :, 3 * QK:PARTS], 0.0).then_inc(S["const_ready"], 1)
            pool.wait_ge(S["const_ready"], 6)
            for m in (ident, identb):
                nc.gpsimd.affine_select(out=m[:, :], in_=m[:, :], compare_op=ALU.not_equal, fill=1.0, base=0,
                                        pattern=[[-1, P]], channel_multiplier=1).then_inc(S["const_ready"], 1)
            nc.gpsimd.affine_select(out=mask[:, :], in_=mask[:, :], compare_op=ALU.is_ge, fill=NEG, base=0,
                                    pattern=[[-1, P]], channel_multiplier=1).then_inc(S["const_ready"], 1)
            nc.gpsimd.memset(v_sb[:, :, :, HD:HD + 1], 1.0).then_inc(S["const_ready"], 1)
            pool.wait_ge(S["const_ready"], 10)
            nc.gpsimd.memset(k_st[ROWS:ROWS + SHIFT, :, :], -1.0).then_inc(S["ones_ready"], 1)
            pool.wait_ge(S["ones_ready"], 1)
            pool.sem_inc(S["base_ready"], PAIRED)
            pool.wait_ge(S["w_in"], 96)
            with pool.Fori(0, NB) as b:
                with pool.Fori(0, PAIRS // 2) as kk:
                    for u in range(2):
                        p = b * PAIRS + kk * 2 + u
                        pool.wait_ge(S["qk_ready"], 2 * p + 2 + CREDIT)
                        pool.wait_ge(S["rot_ready"], p + FIRST)
                        for e in range(2):
                            cos = rope_sb[:, 0, bass.ds(kk * 4 + u * 2 + e, 1), :].rearrange("p t n -> p t n").broadcast_to([P, 2 * QK // HD, HALF])
                            nc.gpsimd.tensor_tensor(rc[:, e, :].rearrange("p (h n) -> p h n", n=HALF),
                                                    qk_sb[:, u, e, :].rearrange("p (h n) -> p h n", n=HALF), cos, ALU.mult).then_inc(S["cos_ready"], 1)
                            sin = rope_sb[:, 1, bass.ds(kk * 4 + u * 2 + e, 1), :].broadcast_to([P, QK // HD, HALF])
                            nc.gpsimd.tensor_tensor(rs[:, e, :].rearrange("p (h m n) -> p h m n", m=2, n=HALF)[:, :, 1, :],
                                                    qk_sb[:, u, e, :].rearrange("p (h m n) -> p h m n", m=2, n=HALF)[:, :, 0, :], sin, ALU.mult).then_inc(S["cos_ready"], 1)
                        for e in range(2):
                            pool.wait_ge(S["ffn_copied"], 2 * p + e + 1 + CREDIT)
                            pool.wait_ge(S["xn_ready"], 2 * p + e + 1 + FIRST)
                            xt = x_sb[:, bass.ds(2 * p + e, 1), :].rearrange("p o n -> p (o n)")
                            nc.gpsimd.tensor_tensor(xt, xt, ffn_sb[:, u, e, :], ALU.add).then_inc(S["base_ready"], 1)
                def one(j, g):
                    banks = banks_before(b, j, g) + 16 * j
                    for i in range(CT):
                        banks = banks + USES[i]
                        pool.wait_ge(S["probs_ready"], banks + CREDIT)
                        pool.sem_inc(S["unit_seen"], 1)
                        blk = prob[:, i % 2, :, i * P:(i + 1) * P]
                        nc.gpsimd.affine_select(out=blk, in_=blk, compare_op=ALU.is_ge, fill=0.0, base=0,
                                                pattern=[[0, R], [1, P]], channel_multiplier=-1).then_inc(S["diag_masked"], 1)
                slots(pool, b, one)

        @block.scalar
        def _(act):
            act.sem_inc(S["xnT_ready"], CREDIT)
            act.sem_inc(S["qk_ready"], CREDIT)
            act.sem_inc(S["v_ready"], CREDIT)
            act.sem_inc(S["ffn_copied"], CREDIT)
            act.sem_inc(S["partsT_ready"], CREDIT)
            act.sem_inc(S["probs_ready"], CREDIT)
            act.sem_inc(S["onT_ready"], CREDIT)
            act.sem_inc(S["o_copied"], FIRST)
            act.wait_ge(S["var_ready"], 1)
            nc.scalar.activation(std[:, 0:TILES], var[:, 0:TILES], ACT.Sqrt).then_inc(S["std_ready"], 1)
            for m in range(2):
                for c in range(KC):
                    act.wait_ge(S["t_acc"], 2 * m + c + 1)
                    nc.scalar.activation(tT[:, m, c, :], psA[:, 2 * m + c, 0:D], ACT.Copy,
                                         scale=(1.0 if m == 0 else -1.0) / D).then_inc(S["t_copied"], 1)
            act.wait_ge(S["w_in"], 96)
            for c in range(KC):
                act.wait_ge(S["m_acc"], c + 1)
                nc.scalar.activation(w_sb[:, c, QKV:QKV + D], psS[:, c, 0:D], ACT.Copy).then_inc(S["m_copied"], 1)

            act.wait_ge(S["var_ready"], 2)
            nc.scalar.activation(std[:, TILES:2 * TILES], var[:, TILES:2 * TILES], ACT.Sqrt).then_inc(S["std_ready"], 1)

            with act.Fori(0, NB) as b:
                def body(kb, u, do_x, do_qk, do_t):
                    if do_x:
                        p = b * PAIRS + kb + u
                        act.wait_ge(S["xn_transposed"], p + 1 + CREDIT)
                        act.wait_ge(S["ffn_ready"], 2 * p - 2 + PAIRED)
                        nc.scalar.activation(xnT[:, u % 2, :, :], psS[:, :, 0:D], ACT.Copy).then_inc(S["xnT_ready"], 1)
                    if do_qk:
                        p = b * PAIRS + kb + u - 1
                        par = (u - 1) % 2
                        t = kb * 2 + 2 * (u - 1)
                        act.wait_ge(S["parts_ready"], p + 1)
                        for e in range(2):
                            act.wait_ge(S["qkv_ready"], 2 * p + e + 1)
                            nc.scalar.activation(v_sb[:, t + e:t + e + 1, :, 0:HD].rearrange("p o g d -> p (o g) d"),
                                                 psA[:, 2 * e, QK:QKV].rearrange("p (g d) -> p g d", g=KV), ACT.Copy).then_inc(S["v_ready"], 1)
                            nc.scalar.activation(qk_sb[:, par, e, :], psA[:, 2 * e, 0:QK], ACT.Copy).then_inc(S["qk_ready"], 1)
                            act.wait_ge(S["base_ready"], 2 * p - 2 + PAIRED)
                            act.wait_ge(S["ffn_ready"], 2 * p + e + 1 + PAIRED)
                            nc.scalar.activation(ffn_sb[:, par, e, :], psA[:, 2 * e + 1, 0:D], ACT.Copy).then_inc(S["ffn_copied"], 1)
                    if do_t:
                        p = b * PAIRS + kb + u - 3
                        lp = u - 3
                        ch = (lp // 2) % 2
                        act.wait_ge(S["parts_stored"], 16 * (b * NJ) + 8 * kb + 16 * (lp // 2 + 1))
                        for e in range(2):
                            act.wait_ge(S["parts_transposed"], 2 * p + e + 1 + PAIRED)
                            i = (2 * lp + e) % CT
                            nc.scalar.activation(pT[:, ch, :, i * P:(i + 1) * P],
                                                 ps_parts[e].rearrange("p (k s) -> p k s", k=BLK), ACT.Copy).then_inc(S["partsT_ready"], 1)

                for k in range(PAIRS + 3):
                    body(k - k % 4, k % 4, k < PAIRS, 1 <= k <= PAIRS, k >= 3)

                def copy_sums(n, unit):
                    act.wait_ge(S["pv_done"], unit + CREDIT)
                    nc.scalar.activation(oraw[:, bass.ds(n, 1), :].rearrange("p o s -> p (o s)"), psO[:, :], ACT.Copy).then_inc(S["o_copied"], 1)

                def one(j, g):
                    last = isinstance(g, int) and 4 * j + g == STEPS - 1
                    bank = banks_before(b, j, g)
                    first = 4 * quads_before(b, j, g)
                    unit = first
                    for q in range(j + 1):
                        for i in range(CT):
                            uses = USES[i] if q == j else 4
                            s0 = i * P if q == j else 0
                            hp = R // uses
                            w = CH - s0
                            act.wait_ge(S["pv_done"], unit + 1)
                            for k in range(uses):
                                act.wait_ge(S["scores_ready"], bank + 1)
                                nc.scalar.activation(prob[:, i % 2, k * hp:(k + 1) * hp, s0:CH],
                                                     score_bank(last, uses, i, k)[:, 0:hp * w].rearrange("p (h s) -> p h s", h=hp),
                                                     ACT.Exp).then_inc(S["probs_ready"], 1)
                                bank = bank + 1
                            if q == 0 and i == 0 and not (isinstance(g, int) and 4 * j + g == 0):
                                copy_sums(4 * j + g - 1, first)
                            unit = unit + 1
                slots(act, b, one)
                copy_sums(STEPS - 1, (b + 1) * 4 * QUADS)

                def onT(j, i):
                    t = b * TILES + 4 * j + i
                    act.wait_ge(S["on_transposed"], t + 1 + CREDIT)
                    act.wait_ge(S["wo_done"], t + 1)
                    nc.scalar.activation(o_nT[:, i % 2, :], psS[:, i % 2, 0:D], ACT.Copy).then_inc(S["onT_ready"], 1)
                with act.Fori(0, NJ) as j:
                    for i in range(CT):
                        onT(j, i)

        @block.vector
        def _(dve):
            dve.sem_inc(S["parts_ready"], CREDIT)
            dve.sem_inc(S["a_reduced"], CREDIT)
            dve.sem_inc(S["o_normed"], CREDIT)
            dve.sem_inc(S["out_ready"], CREDIT)
            for name in ("xn_ready", "rot_ready", "rot_half", "rest_ready", "mpart_ready", "smax_ready"):
                dve.sem_inc(S[name], FIRST)
            dve.wait_ge(S["w_in"], 96)
            nc.vector.memset(bias_p[:, :], 0.0).then_inc(S["bias_step"], 1)
            left = bias_sb
            for k in range(3):
                nc.vector.tensor_copy(bias_c[:, k, :], left[:, :]).then_inc(S["bias_step"], 1)
                dve.wait_ge(S["bias_step"], 2 * k + 2)
                nc.vector.tensor_tensor(bias_r[:, :], left[:, :], bias_c[:, k, :], ALU.subtract).then_inc(S["bias_step"], 1)
                dve.wait_ge(S["bias_step"], 2 * k + 3)
                left = bias_r
                nc.vector.tensor_copy(bias_p[32 * k:32 * k + 1, :], bias_c[32 * k:32 * k + 1, k, :]).then_inc(S["bias_ready"], 1)
            dve.wait_ge(S["table_in"], 48)
            nc.vector.tensor_scalar(wf[:, 2], wf[:, 0], -1.0, None, ALU.mult).then_inc(S["negated"], 1)
            dve.wait_ge(S["w_in"], 96)
            for c in range(KC):
                nc.vector.tensor_scalar(w_sb[:, c, 0:D].rearrange("p (g r d) -> p g r d", g=KV, r=R),
                                        wq_raw[:, c, :].rearrange("p (r g d) -> p g r d", g=KV, r=R),
                                        float(HD) ** -0.5, None, ALU.mult).then_inc(S["wq_scaled"], 1)

            for b in range(NB):
                bt = slice(b * TILES, (b + 1) * TILES)
                for t in range(b * TILES, (b + 1) * TILES):
                    if t % CT == 0:
                        dve.wait_ge(x_in[t // CT % NJ], (b + 1) * 16)
                    nc.vector.bn_stats(bn[:, t, :], x_sb[:, t, :]).then_inc(S["bn_ready"], 1)
                dve.wait_ge(S["bn_ready"], (b + 1) * TILES)
                for t in range(b * TILES, (b + 1) * TILES):
                    nc.vector.bn_aggr(stat[:, t, :], bn[:, t, :]).then_inc(S["stat_ready"], 1)
                dve.wait_ge(S["stat_ready"], (b + 1) * TILES)
                nc.vector.tensor_scalar(var[:, bt], stat[:, bt, 1], EPS, None, ALU.add).then_inc(S["var_ready"], 1)
                dve.wait_ge(S["std_ready"], b + 1)
                nc.vector.reciprocal(tmp[:, bt], std[:, bt]).then_inc(S["newton"], 1)
                dve.wait_ge(S["newton"], 5 * b + 1)
                nc.vector.tensor_tensor(tmp2[:, bt], tmp[:, bt], tmp[:, bt], ALU.mult).then_inc(S["newton"], 1)
                dve.wait_ge(S["newton"], 5 * b + 2)
                nc.vector.tensor_tensor(std[:, bt], tmp2[:, bt], var[:, bt], ALU.mult).then_inc(S["newton"], 1)
                dve.wait_ge(S["newton"], 5 * b + 3)
                nc.vector.tensor_scalar(tmp2[:, bt], std[:, bt], -0.5, 1.5, ALU.mult, ALU.add).then_inc(S["newton"], 1)
                dve.wait_ge(S["newton"], 5 * b + 4)
                nc.vector.tensor_tensor(rstd[:, bt], tmp[:, bt], tmp2[:, bt], ALU.mult).then_inc(S["newton"], 1)
            dve.wait_ge(S["newton"], 5 * NB)
            dve.sem_inc(S["batch_seen"], 1)

            with dve.Fori(0, NB) as b:
                def body(kb, u, do_n, do_r):
                    p = b * PAIRS + kb + u

                    def normalise(e):
                        if e == 0:
                            dve.wait_ge(S["xn_transposed"], p + 1)
                        t = (b * PAIRS + kb) * 2 + (2 * u + e)
                        nc.vector.tensor_scalar(xn[:, u % 2, e, :], x_sb[:, bass.ds(t, 1), :].rearrange("p o n -> p (o n)"),
                                                stat[:, bass.ds(t, 1), 0:1].rearrange("p o n -> p (o n)"), rstd[:, bass.ds(t, 1)],
                                                ALU.subtract, ALU.mult).then_inc(S["xn_ready"], 1)

                    if not do_r:
                        if do_n:
                            normalise(0)
                            normalise(1)
                        return
                    q = p - 3
                    par = (u - 3) % 2
                    halves = lambda t: t.rearrange("p e (h m n) -> p e h m n", m=2, n=HALF)
                    dve.wait_ge(S["qk_ready"], 2 * q + 2 + CREDIT)
                    dve.wait_ge(S["rot_half"], q + FIRST)
                    for e in range(2):
                        sin = rope_sb[:, 1, bass.ds(kb * 2 + 2 * (u - 3) + e, 1), :].broadcast_to([P, QK // HD, HALF])
                        nc.vector.tensor_tensor(halves(rs)[:, e, :, 0, :], halves(qk_sb[:, par])[:, e, :, 1, :], sin, ALU.mult).then_inc(S["sin_ready"], 1)
                    if do_n:
                        normalise(0)
                    dve.wait_ge(S["sin_ready"], 2 * q + 2)
                    dve.wait_ge(S["cos_ready"], 4 * q + 4)
                    dve.wait_ge(S["rest_ready"], q + FIRST)
                    flat = lambda t: t.rearrange("p e (h m n) -> p (e h) m n", m=2, n=HALF)
                    nc.vector.tensor_tensor(flat(rot)[:, :, 0, :], flat(rc)[:, :, 0, :], flat(rs)[:, :, 0, :], ALU.subtract).then_inc(S["rot_half"], 1)
                    nc.vector.tensor_tensor(flat(rot)[:, :, 1, :], flat(rc)[:, :, 1, :], flat(rs)[:, :, 1, :], ALU.add).then_inc(S["rot_ready"], 1)
                    if do_n:
                        normalise(1)
                    dve.wait_ge(S["rot_half"], q + 1 + FIRST)
                    dve.wait_ge(S["rot_ready"], q + 1 + FIRST)
                    dve.wait_ge(S["parts_transposed"], 2 * q - 2 + PAIRED)
                    part = [parts[:, par, :, k * QK:(k + 1) * QK] for k in range(3)]
                    nc.vector.tensor_copy(part[0], rot).then_inc(S["part1_ready"], 1)
                    dve.wait_ge(S["part1_ready"], q + 1)
                    dve.wait_ge(S["parts_ready"], q + CREDIT)
                    nc.vector.tensor_tensor(rest, rot, part[0], ALU.subtract).then_inc(S["rest_ready"], 1)
                    dve.wait_ge(S["rest_ready"], q + 1 + FIRST)
                    nc.vector.tensor_copy(part[1], rest).then_inc(S["part2_ready"], 1)
                    dve.wait_ge(S["part2_ready"], q + 1)
                    nc.vector.tensor_tensor(part[2], rest, part[1], ALU.subtract).then_inc(S["parts_ready"], 1)

                for u in range(3):
                    body(0, u, True, False)
                body(0, 3, True, True)
                with dve.Fori(0, (PAIRS - 4) // 2) as kk:
                    for u in range(2):
                        body(kk * 2, u + 4, True, True)
                for u in range(2):
                    body(PAIRS, u, False, True)
                def reduce(v):
                    n, nq, m = a_use(v)
                    q, i, h2 = m // 8, (m % 8) // 2, m % 2
                    w = (i + 1) * P if q == nq - 1 else CH
                    if m == 0:
                        dve.wait_ge(S["smax_ready"], b * STEPS + n + FIRST)
                    dve.wait_ge(S["a_scores"], b * ALL + v + 1)
                    nc.vector.reduce_max(pmax[:, 2 * h2:2 * h2 + 2, i, q], psA[:, 2 * h2:2 * h2 + 2, 0:w], AX.X).then_inc(S["a_reduced"], 1)
                    if m == 8 * nq - 1:
                        dve.wait_ge(S["a_reduced"], b * ALL + v + 1 + CREDIT)
                        dve.wait_ge(S["smax_transposed"], b * STEPS + n + FIRST)
                        nc.vector.reduce_max(smax[:, :], pmax[:, :, :, 0:nq].rearrange("p r i q -> p (r i) q"), AX.X).then_inc(S["smax_ready"], 1)

                def shift(n):
                    rows = (psS[0:R * CT, 0, 0:P] if n == 0 else psX[0:R * CT, 0:P])
                    n = b * STEPS + n
                    dve.wait_ge(S["smax_transposed"], n + 1 + FIRST)
                    dve.wait_ge(S["shift_in"], n * 16 * SHIFT + LOADED)
                    nc.vector.tensor_copy(mpart[:, 0, :], rows).then_inc(S["mhi_ready"], 1)
                    dve.wait_ge(S["mhi_ready"], n + 1)
                    nc.vector.tensor_tensor(mpart[:, 1, :], rows, mpart[:, 0, :], ALU.subtract).then_inc(S["mpart_ready"], 1)

                for v in range(PRE // 2):
                    reduce(v)
                shift(0)
                body(PAIRS, 2, False, True)
                for v in range(PRE // 2, PRE):
                    reduce(v)
                v = PRE
                for n in range(STEPS):
                    for u in range(4 * (n // KV + 1)):
                        while v < plan[n][u]:
                            reduce(v)
                            v += 1
                        if turn[n][u] is not None:
                            shift(turn[n][u])

                dve.wait_ge(S["base_ready"], (b + 1) * TILES + PAIRED)
                def norm(j, i):
                    t = b * TILES + 4 * j + i
                    dve.wait_ge(S["o_transposed"], t + 1)
                    o = psA[:, i % 2, :].rearrange("p (g r w) -> p g r w", g=KV, r=R)
                    dve.wait_ge(S["o_normed"], t + CREDIT)
                    nc.vector.reciprocal(rl[:, :].rearrange("p (g r o) -> p g r o", g=KV, o=1), o[:, :, :, HD:HD + 1]).then_inc(S["rl_ready"], 1)
                    dve.wait_ge(S["rl_ready"], t + 1)
                    dve.wait_ge(S["on_transposed"], t + 1)
                    nc.vector.tensor_tensor(o_n[:, i % 2, :].rearrange("p (r g d) -> p g r d", r=R, g=KV), o[:, :, :, 0:HD],
                                            rl[:, :].rearrange("p (g r o) -> p g r o", g=KV, o=1).broadcast_to([P, KV, R, HD]),
                                            ALU.mult).then_inc(S["o_normed"], 1)

                def add(j, i):
                    t = b * TILES + 4 * j + i
                    dve.wait_ge(S["wo_done"], t + 1 + CREDIT)
                    xt = x_sb[:, bass.ds(t, 1), :].rearrange("p o n -> p (o n)")
                    nc.vector.tensor_tensor(xt, psA[:, 2 + i % 2, 0:D], xt, ALU.add).then_inc(S["out_ready"], 1)

                for i in range(CT):
                    norm(0, i)
                    if i >= 2:
                        add(0, i - 2)
                with dve.Fori(1, NJ) as j:
                    for i in range(CT):
                        norm(j, i)
                        if i >= 2:
                            add(j, i - 2)
                        else:
                            add(j - 1, i + 2)
                for i in (2, 3):
                    add(NJ - 1, i)

        @block.tensor
        def _(pe):
            mm = nc.tensor.matmul
            pe.sem_inc(S["xn_transposed"], CREDIT)
            pe.sem_inc(S["ffn_ready"], PAIRED)
            pe.sem_inc(S["parts_transposed"], PAIRED)
            pe.sem_inc(S["smax_transposed"], FIRST)
            pe.sem_inc(S["pv_done"], CREDIT)
            pe.sem_inc(S["on_transposed"], CREDIT)
            pe.sem_inc(S["wo_done"], CREDIT)
            pe.wait_ge(S["table_in"], 48)
            pe.wait_ge(S["negated"], 1)
            C, SN = range(NT)
            for m, terms in enumerate((((0, C), (1, SN)), ((1, C), (2, SN)))):
                for c in range(KC):
                    for k, (w, f) in enumerate(terms):
                        for d in range(KC):
                            last = mm(psA[:, 2 * m + c, 0:D], wf[:, w, d, c * P:(c + 1) * P], dft_sb[:, f, d, :],
                                      start=(k == 0 and d == 0), stop=(k == 1 and d == KC - 1))
                    last.then_inc(S["t_acc"], 1)
            pe.wait_ge(S["t_copied"], 4)
            for c in range(KC):
                for m, f in enumerate((C, SN)):
                    for d in range(KC):
                        last = mm(psS[:, c, 0:D], tT[:, m, d, c * P:(c + 1) * P], dft_sb[:, f, d, :],
                                  start=(m == 0 and d == 0), stop=(m == 1 and d == KC - 1))
                last.then_inc(S["m_acc"], 1)
            pe.wait_ge(S["m_copied"], 2)
            pe.wait_ge(S["const_ready"], 10)
            pe.wait_ge(S["ones_ready"], 1)
            pe.wait_ge(S["wq_scaled"], 2)
            pe.wait_ge(S["bias_ready"], 3)

            with pe.Fori(0, NB) as b:
                pe.wait_ge(S["out_ready"], b * TILES + CREDIT)

                def body(kb, u, do_x, do_qkv, do_t):
                    if do_x:
                        p = b * PAIRS + kb + u
                        pe.wait_ge(S["xn_ready"], 2 * p + 2 + FIRST)
                        pe.wait_ge(S["xnT_ready"], p + CREDIT)
                        for e in range(2):
                            for c in range(KC):
                                last = nc.tensor.transpose(psS[:, e, c * P:(c + 1) * P], xn[:, u % 2, e, c * P:(c + 1) * P], ident[:, :])
                        last.then_inc(S["xn_transposed"], 1)
                    if do_qkv:
                        p = b * PAIRS + kb + u - 1
                        par = (u - 1) % 2
                        pe.wait_ge(S["xnT_ready"], p + 1 + CREDIT)
                        for e in range(2):
                            pe.wait_ge(S["qk_ready"], 2 * p + e + 1)
                            pe.wait_ge(S["v_ready"], 2 * p + e + 1)
                            for c in range(KC):
                                last = mm(psA[:, 2 * e, 0:QKV], xnT[:, par, e, c * P:(c + 1) * P], w_sb[:, c, 0:QKV], start=(c == 0), stop=(c == KC - 1))
                            last.then_inc(S["qkv_ready"], 1)
                            pe.wait_ge(S["ffn_copied"], 2 * p + e + 1)
                            mm(psA[:, 2 * e + 1, 0:D], ones[:, :], bias_p[:, :], start=True, stop=False)
                            for c in range(KC):
                                last = mm(psA[:, 2 * e + 1, 0:D], xnT[:, par, e, c * P:(c + 1) * P], w_sb[:, c, QKV:QKV + D], start=False, stop=(c == KC - 1))
                            last.then_inc(S["ffn_ready"], 1)
                    if do_t:
                        p = b * PAIRS + kb + u - 3
                        par = (u - 3) % 2
                        pe.wait_ge(S["parts_ready"], p + 1 + CREDIT)
                        for e in range(2):
                            pe.wait_ge(S["partsT_ready"], 2 * p + e + 1)
                            for k in range(BLK):
                                last = nc.tensor.transpose(ps_parts[e][:, k * P:(k + 1) * P], parts[:, par, e, k * P:(k + 1) * P], identb[:, :])
                            last.then_inc(S["parts_transposed"], 1)

                def a_scores(v):
                    n, nq, m = a_use(v)
                    q, i, h2 = m // 8, (m % 8) // 2, m % 2
                    g = n % KV
                    diag = q == nq - 1
                    w = (i + 1) * P if diag else CH
                    if n % KV == 0 and m == 0:
                        pe.wait_ge(S["stacks_in"], (b * NJ + nq) * 16 * LOADS + LOADED)
                    pe.wait_ge(S["a_reduced"], b * ALL + v + 1)
                    for r in (2 * h2, 2 * h2 + 1):
                        last = mm(psA[:, r, 0:w], q_st[0:ROWS, n, r, i * P:(i + 1) * P], k_st[0:ROWS, g, q * CH:q * CH + w],
                                  start=True, stop=not diag)
                        if diag:
                            last = mm(psA[:, r, w - P:w], identb[:, :], mask[:, :], start=False, stop=True)
                    last.then_inc(S["a_scores"], 1)

                def transpose_max(n):
                    rows = (psS[0:R * CT, 0, 0:P] if n == 0 else psX[0:R * CT, 0:P])
                    pe.wait_ge(S["smax_ready"], b * STEPS + n + 1 + FIRST)
                    pe.wait_ge(S["mpart_ready"], b * STEPS + n + FIRST)
                    nc.tensor.transpose(rows, smax[:, :], ident[:, :]).then_inc(S["smax_transposed"], 1)

                for k in range(PAIRS + 3):
                    body(k - k % 4, k % 4, k < PAIRS, 1 <= k <= PAIRS, k >= 3)
                    if k == PAIRS:
                        for name in ("qk_ready", "v_ready", "ffn_copied"):
                            pe.wait_ge(S[name], (b + 1) * TILES + CREDIT)
                        for v in range(PRE // 2):
                            a_scores(v)
                    if k == PAIRS + 1:
                        transpose_max(0)
                for v in range(PRE // 2, PRE):
                    a_scores(v)
                pe.wait_ge(S["partsT_ready"], (b + 1) * TILES + CREDIT)

                def pv(j, g, u):
                    n = step_of(b, j, g)
                    q, i = u // CT, u % CT
                    s0 = i * P if q == j else 0
                    if u == 0:
                        pe.wait_ge(S["o_copied"], n + FIRST)
                    if q == j:
                        pe.wait_ge(S["diag_masked"], 4 * n + i + 1)
                    else:
                        pe.wait_ge(S["probs_ready"], banks_before(b, j, g) + 4 * (u + 1) + CREDIT)
                    for r in range(R):
                        last = mm(psO[32 * r:32 * r + VW, s0:CH], v_sb[:, u, g, :], prob[:, i % 2, r, s0:CH],
                                  start=(u == 0), stop=(u == 4 * j + 3), tile_position=(0, 32 * r))
                    last.then_inc(S["pv_done"], 1)

                def one(j, g):
                    n = step_of(b, j, g)
                    nl = n_in_batch(j, g)
                    tail = nl == STEPS - 1
                    v = PRE if nl == 0 else plan[nl - 1][-1]
                    bank = banks_before(b, j, g)
                    pe.wait_ge(S["shift_in"], (n + 1) * 16 * SHIFT + LOADED)
                    for u in range(4 * (j + 1)):
                        q, i = u // CT, u % CT
                        uses = USES[i] if q == j else 4
                        s0 = i * P if q == j else 0
                        hp = R // uses
                        w = CH - s0
                        for k in range(uses):
                            if tail and u > 0:
                                pe.wait_ge(S["probs_ready"], bank - 1)
                            elif tail and k >= 2:
                                pe.wait_ge(S["a_reduced"], (b + 1) * ALL + CREDIT)
                            else:
                                pe.wait_ge(S["probs_ready"], bank + 1)
                            for h in range(hp):
                                last = mm(score_bank(tail, uses, i, k)[:, h * w:(h + 1) * w], k_st[0:ROWS + SHIFT, g, u * P:(u + 1) * P],
                                          q_st[0:ROWS + SHIFT, n_in_batch(j, g), k * hp + h, s0:CH], start=True, stop=True)
                            last.then_inc(S["scores_ready"], 1)
                            bank = bank + 1
                            if k == (uses - 1 if tail else 1):
                                if u > 0:
                                    pv(j, g, u - 1)
                                elif n_in_batch(j, g) > 0:
                                    pv(*((j, g - 1, 4 * j + 3) if g > 0 else (j - 1, KV - 1, 4 * j - 1)))
                            if k == 1:
                                while v < plan[nl][u] - 2:
                                    a_scores(v)
                                    v += 1
                        while v < plan[nl][u]:
                            a_scores(v)
                            v += 1
                        if turn[nl][u] is not None:
                            transpose_max(turn[nl][u])
                for n in range(STEPS):
                    one(n // KV, n % KV)
                pv(NJ - 1, KV - 1, TILES - 1)

                pe.wait_ge(S["o_copied"], (b + 1) * STEPS + FIRST)
                pe.wait_ge(S["a_reduced"], (b + 1) * 8 * QUADS + CREDIT)

                def tr_o(j, i):
                    t = b * TILES + 4 * j + i
                    pe.wait_ge(S["o_normed"], t + 1)
                    for g in range(KV):
                        last = nc.tensor.transpose(psA[:, i % 2, g * P:(g + 1) * P],
                                                   oraw[:, 4 * j + g, i * P:(i + 1) * P], ident[:, :])
                    last.then_inc(S["o_transposed"], 1)

                def tr_n(j, i):
                    t = b * TILES + 4 * j + i
                    pe.wait_ge(S["o_normed"], t + 1 + CREDIT)
                    pe.wait_ge(S["onT_ready"], t + 1)
                    for c in range(KC):
                        last = nc.tensor.transpose(psS[:, i % 2, c * P:(c + 1) * P], o_n[:, i % 2, c * P:(c + 1) * P], ident[:, :])
                    last.then_inc(S["on_transposed"], 1)

                def project(j, i):
                    t = b * TILES + 4 * j + i
                    pe.wait_ge(S["onT_ready"], t + 1 + CREDIT)
                    pe.wait_ge(S["out_ready"], t + 1)
                    for c in range(KC):
                        last = mm(psA[:, 2 + i % 2, 0:D], o_nT[:, i % 2, c * P:(c + 1) * P], wo_sb[:, c, :], start=(c == 0), stop=(c == KC - 1))
                    last.then_inc(S["wo_done"], 1)

                for t in range(TILES + 2):
                    if t < TILES:
                        tr_o(t // CT, t % CT)
                    if 1 <= t <= TILES:
                        tr_n((t - 1) // CT, (t - 1) % CT)
                    if t >= 2:
                        project((t - 2) // CT, (t - 2) % CT)


_INS = ["L0_attn_x", "L0_attn_wq", "L0_attn_wk", "L0_attn_wv", "L0_attn_wo",
        "L0_ffn_w_freq_real", "L0_ffn_w_freq_imag", "L0_ffn_bias"]


def kernel(**inputs):
    import numpy as _np
    import concourse.bacc as _bacc
    from concourse import mybir as _mybir
    from concourse.bass_utils import run_bass_kernel_spmd as _run

    nc = _bacc.Bacc("TRN2", target_bir_lowering=False, num_devices=1)
    arrays, args = {}, []

    def give(name, a):
        arrays[name] = a
        args.append(nc.dram_tensor(name, a.shape, _mybir.dt.from_np(a.dtype), kind="ExternalInput").ap())

    for name in _INS:
        give(f"in_{name}", _np.ascontiguousarray(inputs[name]))
    N = 256
    turn = 2.0 * _np.pi * ((_np.arange(N)[:, None] * _np.arange(N)[None, :]) % N) / N
    give("dft_tables", _np.stack([_np.cos(turn), _np.sin(turn)]).astype(_np.float32))
    inv = (1.0 / _np.float32(10000.0) ** (_np.arange(8, dtype=_np.float32) / _np.float32(8))).astype(_np.float32)
    ang = (_np.arange(2048, dtype=_np.float32)[:, None] * inv[None, :]).astype(_np.float32)
    give("rope_tables", _np.stack([_np.cos(ang), _np.sin(ang)]).astype(_np.float32))
    out = nc.dram_tensor("out_0", (2, 2048, 256), _mybir.dt.float32, kind="ExternalOutput").ap()
    attention_fourier_block(nc, *args, out)
    r = _run(nc, [arrays], core_ids=[0])
    return r.results[0]["out_0"]
```

```python
import concourse.bass as bass
from concourse import mybir
from contextlib import ExitStack


def attention_fourier_block(nc, x, wq, wk, wv, wo, w_re, w_im, bias, dft, rope, out):
    fp32 = mybir.dt.float32
    bf16 = mybir.dt.bfloat16
    ALU = mybir.AluOpType
    ACT = mybir.ActivationFunctionType
    AX = mybir.AxisListType

    P = 128
    NB, SEQ, D = x.shape
    KV = 4
    HD = wk.shape[1] // KV
    NH = D // HD
    R = NH // KV
    HALF = HD // 2
    TILES = SEQ // P
    CH = 512
    CT = CH // P
    NJ = SEQ // CH
    STEPS = NJ * KV
    QK = D + KV * HD
    QKV = QK + KV * HD
    KC = D // P
    PAIRS = TILES // 2
    ROWS = 3 * 2 * HD
    SHIFT = 2
    PARTS = 1024
    BLK = PARTS // P
    VW = 32
    LOADS = 12
    NEG = -1.0e30
    EPS = 1e-5
    CREDIT = 2
    PAIRED = 4
    FIRST = 1
    LOADED = 16
    QUADS = KV * NJ * (NJ + 1) // 2
    RING = 3
    USES = ((4, 4, 2, 2), (4, 4, 2, 1), (4, 4, 4, 1), (4, 4, 2, 2))
    BANKS = [16 * j + sum(USES[j]) for j in range(NJ)]

    x_v = x.rearrange("b (t p) d -> p (b t) d", p=P)
    out_v = out.rearrange("b (t p) d -> p (b t) d", p=P)
    scratch = nc.dram_tensor("parts_scratch", [NB * NJ, PARTS, CH], bf16, kind="Internal").ap()

    ctx = ExitStack()
    with ctx:
        def sb(name, shape, dt):
            return ctx.enter_context(nc.sbuf_tensor(name, shape, dt))

        def pb(name, shape, dt):
            return ctx.enter_context(nc.psum_tensor(name, shape, dt))

        def sem(name):
            return ctx.enter_context(nc.semaphore(name))

        x_sb = sb("x_sb", [P, NB * TILES, D], fp32)
        q_st = sb("q_st", [P, STEPS, R, CH], bf16)
        k_st = sb("k_st", [P, KV, SEQ], bf16)
        v_sb = sb("v_sb", [P, TILES, KV, VW], fp32)
        share = sb("share", [P, 12288], fp32)
        prob = share[:, 0:4096].rearrange("p (u r s) -> p u r s", u=2, r=R)
        oraw = share[:, 4096:12288].rearrange("p (n s) -> p n s", n=STEPS)
        pT = share[:, 0:4096].bitcast(bf16).rearrange("p (c k s) -> p c k s", c=2, k=BLK)
        W2 = 2 * QK
        qk_sb = share[:, 4096:4096 + 2 * W2].rearrange("p (u e n) -> p u e n", u=2, e=2)
        rc = share[:, 5376:5376 + W2].rearrange("p (e n) -> p e n", e=2)
        rs = share[:, 6016:6016 + W2].rearrange("p (e n) -> p e n", e=2)
        rot = share[:, 6656:6656 + W2].rearrange("p (e n) -> p e n", e=2)
        rest = share[:, 7296:7296 + W2].rearrange("p (e n) -> p e n", e=2)
        ffn_sb = share[:, 7936:7936 + 4 * D].rearrange("p (u e n) -> p u e n", u=2, e=2)
        NT = 2
        dft_sb = share[:, 0:NT * 512].rearrange("p (m c n) -> p m c n", m=NT, c=KC)
        wf = share[:, 4096:4096 + 1536].rearrange("p (m c n) -> p m c n", m=3, c=KC)
        wq_raw = share[:, 5632:6144].rearrange("p (c n) -> p c n", c=KC)
        tT = share[:, 9216:9216 + 1024].rearrange("p (m c n) -> p m c n", m=2, c=KC)
        xn = sb("xn", [P, 2, 2, D], fp32)
        xnT = sb("xnT", [P, 2, 2, D], fp32)
        parts = sb("parts", [P, 2, 2, PARTS], bf16)
        w_sb = sb("w_sb", [P, KC, QKV + D], fp32)
        wo_sb = sb("wo_sb", [P, KC, D], fp32)
        bias_sb = sb("bias_sb", [P, D], fp32)
        bias_r = sb("bias_r", [P, D], fp32)
        bias_c = sb("bias_c", [P, 3, D], bf16)
        bias_p = sb("bias_p", [P, D], bf16)
        ones = sb("ones", [P, P], bf16)
        rope_sb = sb("rope_sb", [P, 2, TILES, HALF], fp32)
        ident = sb("ident", [P, P], fp32)
        identb = sb("identb", [P, P], bf16)
        mask = sb("mask", [P, CH], fp32)
        maskb = sb("maskb", [P, P], bf16)
        o_n = sb("o_n", [P, 2, D], fp32)
        o_nT = sb("o_nT", [P, 2, D], fp32)
        bn = sb("bn", [P, NB * TILES, 6], fp32)
        stat = sb("stat", [P, NB * TILES, 2], fp32)
        var = sb("var", [P, NB * TILES], fp32)
        std = sb("std", [P, NB * TILES], fp32)
        rstd = sb("rstd", [P, NB * TILES], fp32)
        tmp = sb("tmp", [P, NB * TILES], fp32)
        tmp2 = sb("tmp2", [P, NB * TILES], fp32)
        pmax = sb("pmax", [P, R, CT, NJ], fp32)
        smax = sb("smax", [P, R * CT], fp32)
        spart = sb("spart", [P, SHIFT, R * CT], bf16)
        spartT = sb("spartT", [P, SHIFT * R * CT], bf16)
        rl = sb("rl", [P, NH], fp32)

        psA = pb("psA", [P, 4, 512], fp32)
        psS = pb("psS", [P, RING, 512], fp32)
        psO = pb("psO", [P, 512], fp32)
        ps_parts = [psO[:, :].bitcast(bf16), psS[:, 2, :].bitcast(bf16)]

        S = {n: sem(n) for n in (
            "w_in", "bias_in", "table_in", "const_ready", "ones_ready", "negated", "wq_scaled", "t_acc", "t_copied", "m_acc", "m_copied",
            "bn_ready", "stat_ready", "var_ready", "std_ready", "newton",
            "xn_ready", "xn_transposed", "xnT_ready", "qkv_ready", "ffn_ready", "qk_ready", "v_ready",
            "ffn_copied", "base_ready", "bias_step", "bias_ready", "cos_ready", "sin_ready", "rot_ready", "part1_ready", "rest_ready",
            "part2_ready", "rot_half", "parts_ready", "parts_transposed", "partsT_ready", "parts_stored", "stacks_in",
            "a_scores", "a_reduced", "smax_ready", "spart1_ready", "spart2_ready", "spartT_ready", "shift_in",
            "scores_ready", "probs_ready", "diag_masked", "pv_done", "o_copied",
            "o_transposed", "rl_ready", "o_normed", "on_transposed", "onT_ready", "wo_done", "out_ready", "out_stored",
            "unit_seen", "stats_seen", "scores_seen")}

        x_in = [sem(f"x_in{c}") for c in range(NJ)]

        def quads_before(b, j, g):
            return b * QUADS + 2 * j * (j + 1) + g * (j + 1)

        def step_of(b, j, g):
            return b * STEPS + 4 * j + g

        def n_in_batch(j, g):
            return 4 * j + g

        def banks_before(b, j, g):
            return b * KV * sum(BANKS) + KV * sum(BANKS[:j]) + g * BANKS[j]

        def slots(engine, b, one):
            for j in range(NJ):
                low = 1 if j == 0 else 0
                high = KV - 1 if j == NJ - 1 else KV
                if low:
                    one(j, 0)
                with engine.Fori(low, high) as g:
                    one(j, g)
                if high < KV:
                    one(j, KV - 1)

        PE_MASKS = 2 * KV

        def on_pe(n, q):
            return q == n // KV and n < PE_MASKS

        def units(j):
            found, banks = [], 0
            for i in range(CT):
                part = [j * i + f for f in range(j)]
                part.insert(j // 2, TILES + i)
                for u in part:
                    diag = u - TILES if u >= TILES else None
                    count = R if diag is None else USES[j][diag]
                    banks += count
                    found.append((u if diag is None else CT * j + diag, 0 if diag is None else diag * P, count, banks, diag))
            return found

        def a_uses(j):
            full = [((2 * h, 2 * h + 1), i, q) for q in range(j) for i in range(CT) for h in range(2)]
            diag = [(range(R), 0, j), (range(R), 1, j)] + [((2 * h, 2 * h + 1), i, j) for i in (2, 3) for h in range(2)]
            order, taken = [], 0
            for k, use in enumerate(diag):
                upto = (k + 1) * len(full) // len(diag)
                order += full[taken:upto] + [use]
                taken = upto
            return order

        A_USES = [(n, m, len(a_uses(n // KV)), use) for n in range(STEPS) for m, use in enumerate(a_uses(n // KV))]
        ALL = len(A_USES)

        SLACK = 3.0
        LAST_SLACK = 0.5
        PRE = 2 * len(a_uses(0))
        FIXED = 0.1

        def a_weight(v):
            heads, i, q = A_USES[v][3]
            return 1.0 if q < A_USES[v][0] // KV else len(heads) * (FIXED + (i + 1) / CT) / 2

        def b_weight(n, u):
            return FIXED + (1 - FIXED) * (1 - units(n // KV)[u][1] / CH)

        dates = []
        begins, total = 0.0, 0.0
        for n in range(STEPS):
            nq = n // KV + 1
            total += sum(a_weight(v) for v in range(ALL) if A_USES[v][0] == n)
            if n > 1:
                dates.append((begins - SLACK - (LAST_SLACK if n == STEPS - 1 else 0.0), total))
            begins += sum(b_weight(n, u) for u in range(4 * nq))
        plan = []
        at, done, spent = PRE, sum(a_weight(v) for v in range(PRE)), 0.0
        aim = done
        for n in range(STEPS):
            plan.append([])
            for u in range(4 * (n // KV + 1)):
                w = b_weight(n, u)
                rate = max([(need - aim) / max(date - spent, w) for date, need in dates if need > aim + 1e-9], default=0.0)
                aim += rate * w
                spent += w
                while at < ALL and done + a_weight(at) <= aim + 0.01:
                    done += a_weight(at)
                    at += 1
                plan[-1].append(at)
        assert at == ALL
        for n in range(1, STEPS):
            assert plan[n - 1][-1] > max(v for v in range(ALL) if A_USES[v][0] == n)

        def score_bank(tail, k):
            if tail:
                return psA[:, k % 5 - RING, :] if k % 5 >= RING else psS[:, k % 5, :]
            return psS[:, k % RING, :]

        EARLY = {2: (1,), 3: (1, 2)}
        PV_AT = 2
        PV_LATE = 3

        def early(uses, k):
            return EARLY[min(uses, 3)].count(k) if uses >= 2 else 0

        block = ctx.enter_context(nc.Block())

        @block.sync
        def _(sp):
            def load_x(b):
                for c in range(NJ):
                    t0 = b * TILES + c * CT
                    sp.dma_start(x_sb[:, t0:t0 + CT, :], x_v[:, t0:t0 + CT, :]).then_inc(x_in[c], 16)

            def load_shift(b, n):
                sp.wait_ge(S["spartT_ready"], b * STEPS + n + 1 + FIRST)
                rows = q_st[ROWS:ROWS + SHIFT, n, :, :].rearrange("o r (i k s) -> o (r i) k s", i=CT, k=CT)
                for k in range(CT):
                    sp.dma_start(rows[:, :, k, :], spartT[32 * k:32 * (k + 1), :]).then_inc(S["shift_in"], 16)

            sp.dma_start(dft_sb, dft.rearrange("m (c p) n -> p m c n", p=P)).then_inc(S["table_in"], 16)
            sp.dma_start(wf[:, 0], w_re.rearrange("(c p) n -> p c n", p=P)).then_inc(S["table_in"], 16)
            sp.dma_start(wf[:, 1], w_im.rearrange("(c p) n -> p c n", p=P)).then_inc(S["table_in"], 16)
            sp.dma_start(bias_sb[:, :], bias.rearrange("(a n) -> a n", a=1).broadcast_to([P, D])).then_inc(S["bias_in"], 16)
            load_x(0)
            sp.dma_start(wq_raw, wq.rearrange("(c p) n -> p c n", p=P)).then_inc(S["w_in"], 16)
            sp.dma_start(w_sb[:, :, D:QK], wk.rearrange("(c p) n -> p c n", p=P)).then_inc(S["w_in"], 16)
            sp.dma_start(w_sb[:, :, QK:QKV], wv.rearrange("(c p) n -> p c n", p=P)).then_inc(S["w_in"], 16)
            sp.dma_start(rope_sb[:, :, :, :], rope.rearrange("m (t p) n -> p m t n", p=P)).then_inc(S["w_in"], 16)
            sp.dma_start(wo_sb[:, :, :], wo.rearrange("(c p) n -> p c n", p=P)).then_inc(S["w_in"], 16)
            for c in range(NJ):
                sp.wait_ge(x_in[c], 16)
            load_x(1)
            sp.sem_inc(S["parts_stored"], CREDIT * 16)
            sp.sem_inc(S["stacks_in"], LOADED)
            sp.sem_inc(S["shift_in"], LOADED)

            with sp.Fori(0, NB) as b:
                for c in range(NJ):
                    cc = b * NJ + c
                    sp.wait_ge(S["partsT_ready"], (cc + 1) * CT + CREDIT)
                    sp.dma_start(scratch[cc].rearrange("(k p) s -> p k s", p=P), pT[:, c % 2]).then_inc(S["parts_stored"], 16)
                    if c == NJ - 1:
                        load_shift(b, 0)
                    sp.wait_ge(S["parts_stored"], (cc + 1 + CREDIT) * 16)
                    sp.wait_ge(S["pv_done"], b * 4 * QUADS + CREDIT)
                    sp.wait_ge(S["stacks_in"], cc * 16 * LOADS + LOADED)
                    for row, part in enumerate((0, 0, 1, 1, 0, 2)):
                        sp.dma_start(q_st[row * HD:(row + 1) * HD, c * KV:(c + 1) * KV, :, :].rearrange("d g r s -> d (g r) s"),
                                     scratch[cc, part * QK:part * QK + D, :].rearrange("(h d) s -> d h s", h=NH)).then_inc(S["stacks_in"], 16)
                    for row, part in enumerate((0, 1, 0, 1, 2, 0)):
                        sp.dma_start(k_st[row * HD:(row + 1) * HD, :, c * CH:(c + 1) * CH],
                                     scratch[cc, part * QK + D:(part + 1) * QK, :].rearrange("(g d) s -> d g s", g=KV)).then_inc(S["stacks_in"], 16)
                with sp.Fori(1, STEPS) as n:
                    load_shift(b, n)
                with sp.Fori(0, NJ) as j:
                    sp.wait_ge(S["out_ready"], b * TILES + j * CT + CT + CREDIT)
                    sp.dma_start(out_v[:, bass.ds(b * TILES + j * CT, CT), :], x_sb[:, bass.ds(b * TILES + j * CT, CT), :]).then_inc(S["out_stored"], 16)
            sp.wait_ge(S["out_stored"], NB * NJ * 16)

        @block.gpsimd
        def _(pool):
            nc.gpsimd.memset(ident[:, :], 0.0).then_inc(S["const_ready"], 1)
            nc.gpsimd.memset(identb[:, :], 0.0).then_inc(S["const_ready"], 1)
            nc.gpsimd.memset(maskb[:, :], 0.0).then_inc(S["const_ready"], 1)
            nc.gpsimd.memset(mask[:, :], 0.0).then_inc(S["const_ready"], 1)
            nc.gpsimd.memset(v_sb[:, :, :, :], 0.0).then_inc(S["const_ready"], 1)
            nc.gpsimd.memset(ones[:, :], 1.0).then_inc(S["const_ready"], 1)
            nc.gpsimd.memset(parts[:, :, :, 3 * QK:PARTS], 0.0).then_inc(S["const_ready"], 1)
            pool.wait_ge(S["const_ready"], 7)
            for m in (ident, identb):
                nc.gpsimd.affine_select(out=m[:, :], in_=m[:, :], compare_op=ALU.not_equal, fill=1.0, base=0,
                                        pattern=[[-1, P]], channel_multiplier=1).then_inc(S["const_ready"], 1)
            nc.gpsimd.affine_select(out=mask[:, :], in_=mask[:, :], compare_op=ALU.is_ge, fill=NEG, base=CH - P,
                                    pattern=[[-1, CH]], channel_multiplier=1).then_inc(S["const_ready"], 1)
            nc.gpsimd.affine_select(out=maskb[:, :], in_=maskb[:, :], compare_op=ALU.is_ge, fill=NEG, base=0,
                                    pattern=[[-1, P]], channel_multiplier=1).then_inc(S["const_ready"], 1)
            nc.gpsimd.memset(v_sb[:, :, :, HD:HD + 1], 1.0).then_inc(S["const_ready"], 1)
            pool.wait_ge(S["const_ready"], 12)
            nc.gpsimd.memset(k_st[ROWS:ROWS + SHIFT, :, :], -1.0).then_inc(S["ones_ready"], 1)
            pool.wait_ge(S["ones_ready"], 1)
            pool.sem_inc(S["base_ready"], PAIRED)
            pool.wait_ge(S["w_in"], 80)
            with pool.Fori(0, NB) as b:
                with pool.Fori(0, PAIRS // 2) as kk:
                    for u in range(2):
                        p = b * PAIRS + kk * 2 + u
                        pool.wait_ge(S["qk_ready"], 2 * p + 2 + CREDIT)
                        pool.wait_ge(S["rot_ready"], p + FIRST)
                        for e in range(2):
                            cos = rope_sb[:, 0, bass.ds(kk * 4 + u * 2 + e, 1), :].rearrange("p t n -> p t n").broadcast_to([P, 2 * QK // HD, HALF])
                            nc.gpsimd.tensor_tensor(rc[:, e, :].rearrange("p (h n) -> p h n", n=HALF),
                                                    qk_sb[:, u, e, :].rearrange("p (h n) -> p h n", n=HALF), cos, ALU.mult).then_inc(S["cos_ready"], 1)
                            sin = rope_sb[:, 1, bass.ds(kk * 4 + u * 2 + e, 1), :].broadcast_to([P, QK // HD, HALF])
                            nc.gpsimd.tensor_tensor(rs[:, e, :].rearrange("p (h m n) -> p h m n", m=2, n=HALF)[:, :, 1, :],
                                                    qk_sb[:, u, e, :].rearrange("p (h m n) -> p h m n", m=2, n=HALF)[:, :, 0, :], sin, ALU.mult).then_inc(S["cos_ready"], 1)
                        for e in range(2):
                            pool.wait_ge(S["ffn_copied"], 2 * p + e + 1 + CREDIT)
                            pool.wait_ge(S["xn_ready"], 2 * p + e + 1 + FIRST)
                            xt = x_sb[:, bass.ds(2 * p + e, 1), :].rearrange("p o n -> p (o n)")
                            nc.gpsimd.tensor_tensor(xt, xt, ffn_sb[:, u, e, :], ALU.add).then_inc(S["base_ready"], 1)
                def one(j, g):
                    for u, (_, s0, _, banks, diag) in enumerate(units(j)):
                        if diag is None:
                            continue
                        pool.wait_ge(S["probs_ready"], banks_before(b, j, g) + banks + RING)
                        pool.sem_inc(S["unit_seen"], 1)
                        blk = prob[:, u % 2, :, s0:s0 + P]
                        nc.gpsimd.affine_select(out=blk, in_=blk, compare_op=ALU.is_ge, fill=0.0, base=0,
                                                pattern=[[0, R], [1, P]], channel_multiplier=-1).then_inc(S["diag_masked"], 1)
                slots(pool, b, one)

        @block.scalar
        def _(act):
            act.sem_inc(S["xnT_ready"], CREDIT)
            act.sem_inc(S["qk_ready"], CREDIT)
            act.sem_inc(S["v_ready"], CREDIT)
            act.sem_inc(S["ffn_copied"], CREDIT)
            act.sem_inc(S["partsT_ready"], CREDIT)
            act.sem_inc(S["probs_ready"], RING)
            act.sem_inc(S["onT_ready"], CREDIT)
            act.sem_inc(S["o_copied"], FIRST)
            for m in range(2):
                for c in range(KC):
                    act.wait_ge(S["t_acc"], 2 * m + c + 1)
                    nc.scalar.activation(tT[:, m, c, :], psA[:, 2 * m + c, 0:D], ACT.Copy,
                                         scale=(1.0 if m == 0 else -1.0) / D).then_inc(S["t_copied"], 1)
            act.wait_ge(S["var_ready"], 1)
            nc.scalar.activation(std[:, 0:TILES], var[:, 0:TILES], ACT.Sqrt).then_inc(S["std_ready"], 1)
            act.wait_ge(S["w_in"], 80)
            for c in range(KC):
                act.wait_ge(S["m_acc"], c + 1)
                nc.scalar.activation(w_sb[:, c, QKV:QKV + D], psS[:, c, 0:D], ACT.Copy).then_inc(S["m_copied"], 1)

            with act.Fori(0, NB) as b:
                def body(kb, u, do_x, do_qk, do_t):
                    if do_x:
                        p = b * PAIRS + kb + u
                        act.wait_ge(S["xn_transposed"], p + 1 + CREDIT)
                        act.wait_ge(S["ffn_ready"], 2 * p - 2 + PAIRED)
                        nc.scalar.activation(xnT[:, u % 2, :, :], psS[:, 0:2, 0:D], ACT.Copy).then_inc(S["xnT_ready"], 1)
                    if do_qk:
                        p = b * PAIRS + kb + u - 1
                        par = (u - 1) % 2
                        t = kb * 2 + 2 * (u - 1)
                        act.wait_ge(S["parts_ready"], p + 1)
                        for e in range(2):
                            act.wait_ge(S["qkv_ready"], 2 * p + e + 1)
                            nc.scalar.activation(v_sb[:, t + e:t + e + 1, :, 0:HD].rearrange("p o g d -> p (o g) d"),
                                                 psA[:, 2 * e, QK:QKV].rearrange("p (g d) -> p g d", g=KV), ACT.Copy).then_inc(S["v_ready"], 1)
                            nc.scalar.activation(qk_sb[:, par, e, :], psA[:, 2 * e, 0:QK], ACT.Copy).then_inc(S["qk_ready"], 1)
                            act.wait_ge(S["base_ready"], 2 * p - 2 + PAIRED)
                            act.wait_ge(S["ffn_ready"], 2 * p + e + 1 + PAIRED)
                            nc.scalar.activation(ffn_sb[:, par, e, :], psA[:, 2 * e + 1, 0:D], ACT.Copy).then_inc(S["ffn_copied"], 1)
                    if do_t:
                        p = b * PAIRS + kb + u - 3
                        lp = u - 3
                        ch = (lp // 2) % 2
                        act.wait_ge(S["parts_stored"], 16 * (b * NJ) + 8 * kb + 16 * (lp // 2 + 1))
                        for e in range(2):
                            act.wait_ge(S["parts_transposed"], 2 * p + e + 1 + PAIRED)
                            i = (2 * lp + e) % CT
                            nc.scalar.activation(pT[:, ch, :, i * P:(i + 1) * P],
                                                 ps_parts[e].rearrange("p (k s) -> p k s", k=BLK), ACT.Copy).then_inc(S["partsT_ready"], 1)

                for k in range(PAIRS + 3):
                    body(k - k % 4, k % 4, k < PAIRS, 1 <= k <= PAIRS, k >= 3)

                def copy_sums(n, unit):
                    act.wait_ge(S["pv_done"], unit + CREDIT)
                    nc.scalar.activation(oraw[:, bass.ds(n, 1), :].rearrange("p o s -> p (o s)"), psO[:, :], ACT.Copy).then_inc(S["o_copied"], 1)

                def one(j, g):
                    tail = isinstance(g, int) and 4 * j + g == STEPS - 1
                    first = 4 * quads_before(b, j, g)
                    for u, (_, s0, count, banks, _) in enumerate(units(j)):
                        hp = R // count
                        w = CH - s0
                        act.wait_ge(S["pv_done"], first + u + 1)
                        for k in range(count):
                            bank = banks - count + k
                            act.wait_ge(S["scores_ready"], banks_before(b, j, g) + bank + 1)
                            nc.scalar.activation(prob[:, u % 2, k * hp:(k + 1) * hp, s0:CH],
                                                 score_bank(tail, bank)[:, 0:hp * w].rearrange("p (h s) -> p h s", h=hp),
                                                 ACT.Exp).then_inc(S["probs_ready"], 1)
                        if u == 0 and not (isinstance(g, int) and 4 * j + g == 0):
                            copy_sums(4 * j + g - 1, first)
                act.wait_ge(S["parts_stored"], ((b + 1) * NJ + CREDIT) * 16)
                slots(act, b, one)
                copy_sums(STEPS - 1, (b + 1) * 4 * QUADS)

                act.wait_ge(S["var_ready"], b + 2)
                nc.scalar.activation(std[:, TILES:2 * TILES], var[:, TILES:2 * TILES], ACT.Sqrt).then_inc(S["std_ready"], 1)

                def onT(j, i):
                    t = b * TILES + 4 * j + i
                    act.wait_ge(S["on_transposed"], t + 1 + CREDIT)
                    act.wait_ge(S["wo_done"], t + 1)
                    nc.scalar.activation(o_nT[:, i % 2, :], psS[:, i % 2, 0:D], ACT.Copy).then_inc(S["onT_ready"], 1)
                with act.Fori(0, NJ) as j:
                    for i in range(CT):
                        onT(j, i)

        @block.vector
        def _(dve):
            dve.sem_inc(S["parts_ready"], CREDIT)
            dve.sem_inc(S["a_reduced"], CREDIT)
            dve.sem_inc(S["o_normed"], CREDIT)
            dve.sem_inc(S["out_ready"], CREDIT)
            for name in ("xn_ready", "rot_ready", "rot_half", "rest_ready", "spart1_ready", "spart2_ready", "spartT_ready", "smax_ready"):
                dve.sem_inc(S[name], FIRST)
            dve.wait_ge(S["table_in"], 48)
            nc.vector.tensor_scalar(wf[:, 2], wf[:, 0], -1.0, None, ALU.mult).then_inc(S["negated"], 1)

            def moments(batch, done):
                bt = slice(batch * TILES, (batch + 1) * TILES)
                for t in range(batch * TILES, (batch + 1) * TILES):
                    if t % CT == 0:
                        dve.wait_ge(x_in[t // CT % NJ], (batch + 1) * 16)
                    nc.vector.bn_stats(bn[:, t, :], x_sb[:, t, :]).then_inc(S["bn_ready"], 1)
                dve.wait_ge(S["bn_ready"], (done + 1) * TILES)
                dve.sem_inc(S["stats_seen"], 1)
                for t in range(batch * TILES, (batch + 1) * TILES):
                    nc.vector.bn_aggr(stat[:, t, :], bn[:, t, :]).then_inc(S["stat_ready"], 1)
                dve.wait_ge(S["stat_ready"], (done + 1) * TILES)
                dve.sem_inc(S["stats_seen"], 1)
                nc.vector.tensor_scalar(var[:, bt], stat[:, bt, 1], EPS, None, ALU.add).then_inc(S["var_ready"], 1)

            def newton(batch, done):
                bt = slice(batch * TILES, (batch + 1) * TILES)
                dve.wait_ge(S["std_ready"], done + 1)
                dve.sem_inc(S["stats_seen"], 1)
                nc.vector.reciprocal(tmp[:, bt], std[:, bt]).then_inc(S["newton"], 1)
                dve.wait_ge(S["newton"], 5 * done + 1)
                nc.vector.tensor_tensor(tmp2[:, bt], tmp[:, bt], tmp[:, bt], ALU.mult).then_inc(S["newton"], 1)
                dve.wait_ge(S["newton"], 5 * done + 2)
                nc.vector.tensor_tensor(std[:, bt], tmp2[:, bt], var[:, bt], ALU.mult).then_inc(S["newton"], 1)
                dve.wait_ge(S["newton"], 5 * done + 3)
                dve.sem_inc(S["stats_seen"], 1)
                nc.vector.tensor_scalar(tmp2[:, bt], std[:, bt], -0.5, 1.5, ALU.mult, ALU.add).then_inc(S["newton"], 1)
                dve.wait_ge(S["newton"], 5 * done + 4)
                nc.vector.tensor_tensor(rstd[:, bt], tmp[:, bt], tmp2[:, bt], ALU.mult).then_inc(S["newton"], 1)

            dve.wait_ge(S["bias_in"], 16)
            nc.vector.memset(bias_p[:, :], 0.0).then_inc(S["bias_step"], 1)
            left = bias_sb
            for k in range(3):
                nc.vector.tensor_copy(bias_c[:, k, :], left[:, :]).then_inc(S["bias_step"], 1)
                dve.wait_ge(S["bias_step"], 2 * k + 2)
                nc.vector.tensor_tensor(bias_r[:, :], left[:, :], bias_c[:, k, :], ALU.subtract).then_inc(S["bias_step"], 1)
                dve.wait_ge(S["bias_step"], 2 * k + 3)
                left = bias_r
                nc.vector.tensor_copy(bias_p[32 * k:32 * k + 1, :], bias_c[32 * k:32 * k + 1, k, :]).then_inc(S["bias_ready"], 1)

            moments(0, 0)
            dve.wait_ge(S["w_in"], 80)
            for c in range(KC):
                nc.vector.tensor_scalar(w_sb[:, c, 0:D].rearrange("p (g r d) -> p g r d", g=KV, r=R),
                                        wq_raw[:, c, :].rearrange("p (r g d) -> p g r d", g=KV, r=R),
                                        float(HD) ** -0.5, None, ALU.mult).then_inc(S["wq_scaled"], 1)

            newton(0, 0)

            with dve.Fori(0, NB) as b:
                dve.wait_ge(S["newton"], 5 * (b + 1))
                dve.sem_inc(S["stats_seen"], 1)

                def body(kb, u, do_n, do_r):
                    p = b * PAIRS + kb + u

                    def normalise(e):
                        if e == 0:
                            dve.wait_ge(S["xn_transposed"], p + 1)
                        t = (b * PAIRS + kb) * 2 + (2 * u + e)
                        nc.vector.tensor_scalar(xn[:, u % 2, e, :], x_sb[:, bass.ds(t, 1), :].rearrange("p o n -> p (o n)"),
                                                stat[:, bass.ds(t, 1), 0:1].rearrange("p o n -> p (o n)"), rstd[:, bass.ds(t, 1)],
                                                ALU.subtract, ALU.mult).then_inc(S["xn_ready"], 1)

                    if not do_r:
                        if do_n:
                            normalise(0)
                            normalise(1)
                        return
                    q = p - 3
                    par = (u - 3) % 2
                    halves = lambda t: t.rearrange("p e (h m n) -> p e h m n", m=2, n=HALF)
                    dve.wait_ge(S["qk_ready"], 2 * q + 2 + CREDIT)
                    dve.wait_ge(S["rot_half"], q + FIRST)
                    for e in range(2):
                        sin = rope_sb[:, 1, bass.ds(kb * 2 + 2 * (u - 3) + e, 1), :].broadcast_to([P, QK // HD, HALF])
                        nc.vector.tensor_tensor(halves(rs)[:, e, :, 0, :], halves(qk_sb[:, par])[:, e, :, 1, :], sin, ALU.mult).then_inc(S["sin_ready"], 1)
                    if do_n:
                        normalise(0)
                    dve.wait_ge(S["sin_ready"], 2 * q + 2)
                    dve.wait_ge(S["cos_ready"], 4 * q + 4)
                    dve.wait_ge(S["rest_ready"], q + FIRST)
                    flat = lambda t: t.rearrange("p e (h m n) -> p (e h) m n", m=2, n=HALF)
                    nc.vector.tensor_tensor(flat(rot)[:, :, 0, :], flat(rc)[:, :, 0, :], flat(rs)[:, :, 0, :], ALU.subtract).then_inc(S["rot_half"], 1)
                    nc.vector.tensor_tensor(flat(rot)[:, :, 1, :], flat(rc)[:, :, 1, :], flat(rs)[:, :, 1, :], ALU.add).then_inc(S["rot_ready"], 1)
                    if do_n:
                        normalise(1)
                    dve.wait_ge(S["rot_half"], q + 1 + FIRST)
                    dve.wait_ge(S["rot_ready"], q + 1 + FIRST)
                    dve.wait_ge(S["parts_transposed"], 2 * q - 2 + PAIRED)
                    part = [parts[:, par, :, k * QK:(k + 1) * QK] for k in range(3)]
                    nc.vector.tensor_copy(part[0], rot).then_inc(S["part1_ready"], 1)
                    dve.wait_ge(S["part1_ready"], q + 1)
                    dve.wait_ge(S["parts_ready"], q + CREDIT)
                    nc.vector.tensor_tensor(rest, rot, part[0], ALU.subtract).then_inc(S["rest_ready"], 1)
                    dve.wait_ge(S["rest_ready"], q + 1 + FIRST)
                    nc.vector.tensor_copy(part[1], rest).then_inc(S["part2_ready"], 1)
                    dve.wait_ge(S["part2_ready"], q + 1)
                    nc.vector.tensor_tensor(part[2], rest, part[1], ALU.subtract).then_inc(S["parts_ready"], 1)

                for u in range(3):
                    body(0, u, True, False)
                body(0, 3, True, True)
                with dve.Fori(0, (PAIRS - 4) // 2) as kk:
                    for u in range(2):
                        body(kk * 2, u + 4, True, True)
                for u in range(3):
                    body(PAIRS, u, False, True)
                def reduce(v):
                    n, m, count, (heads, i, q) = A_USES[v]
                    two = 2 * (v % 2)
                    if m == 0:
                        dve.wait_ge(S["smax_ready"], b * STEPS + n + FIRST)
                    dve.wait_ge(S["a_scores"], b * ALL + v + 1)
                    w = (i + 1) * P
                    per = len(heads) // 2
                    if on_pe(n, q):
                        nc.vector.reduce_max(pmax[:, heads[0]:heads[-1] + 1, i, q].rearrange("p (o h) -> p o h", h=per),
                                             psA[:, two:two + 2, 0:per * w].rearrange("p o (h s) -> p o h s", h=per),
                                             AX.X).then_inc(S["a_reduced"], 1)
                    elif q == n // KV:
                        dve.sem_inc(S["scores_seen"], 1)
                        for k, r in enumerate(heads):
                            scores = psA[:, two + k // per, (k % per) * w:(k % per + 1) * w]
                            last = nc.vector.tensor_tensor_reduce(scores, scores, mask[:, CH - w:CH], 1.0, NEG,
                                                                  ALU.add, ALU.max, pmax[:, r, i, q:q + 1])
                        last.then_inc(S["a_reduced"], 1)
                    else:
                        nc.vector.reduce_max(pmax[:, heads[0]:heads[0] + 2, i, q], psA[:, two:two + 2, :], AX.X).then_inc(S["a_reduced"], 1)
                    if m == count - 1:
                        dve.wait_ge(S["a_reduced"], b * ALL + v + 1 + CREDIT)
                        shift(n, b * STEPS + n)

                def shift(nl, n):
                    dve.wait_ge(S["spart2_ready"], n + FIRST)
                    nc.vector.reduce_max(smax[:, :], pmax[:, :, :, 0:nl // KV + 1].rearrange("p r i q -> p (r i) q"), AX.X).then_inc(S["smax_ready"], 1)
                    dve.wait_ge(S["smax_ready"], n + 1 + FIRST)
                    dve.wait_ge(S["spartT_ready"], n + FIRST)
                    nc.vector.tensor_copy(spart[:, 0, :], smax[:, :]).then_inc(S["spart1_ready"], 1)
                    dve.wait_ge(S["spart1_ready"], n + 1 + FIRST)
                    nc.vector.tensor_tensor(spart[:, 1, :], smax[:, :], spart[:, 0, :], ALU.subtract).then_inc(S["spart2_ready"], 1)
                    dve.wait_ge(S["spart2_ready"], n + 1 + FIRST)
                    dve.wait_ge(S["shift_in"], n * 16 * CT + LOADED)
                    nc.vector.transpose(spartT[:, :], spart[:, :, :].rearrange("p k c -> p (k c)")).then_inc(S["spartT_ready"], 1)

                for v in range(PRE):
                    reduce(v)
                v = PRE
                for n in range(STEPS):
                    for u in range(4 * (n // KV + 1)):
                        while v < plan[n][u]:
                            reduce(v)
                            v += 1

                moments(1, b + 1)

                dve.wait_ge(S["base_ready"], (b + 1) * TILES + PAIRED)
                def norm(j, i):
                    t = b * TILES + 4 * j + i
                    dve.wait_ge(S["o_transposed"], t + 1)
                    o = psA[:, i % 2, :].rearrange("p (g r w) -> p g r w", g=KV, r=R)
                    dve.wait_ge(S["o_normed"], t + CREDIT)
                    nc.vector.reciprocal(rl[:, :].rearrange("p (g r o) -> p g r o", g=KV, o=1), o[:, :, :, HD:HD + 1]).then_inc(S["rl_ready"], 1)
                    dve.wait_ge(S["rl_ready"], t + 1)
                    dve.wait_ge(S["on_transposed"], t + 1)
                    nc.vector.tensor_tensor(o_n[:, i % 2, :].rearrange("p (r g d) -> p g r d", r=R, g=KV), o[:, :, :, 0:HD],
                                            rl[:, :].rearrange("p (g r o) -> p g r o", g=KV, o=1).broadcast_to([P, KV, R, HD]),
                                            ALU.mult).then_inc(S["o_normed"], 1)

                def add(j, i):
                    t = b * TILES + 4 * j + i
                    dve.wait_ge(S["wo_done"], t + 1 + CREDIT)
                    xt = x_sb[:, bass.ds(t, 1), :].rearrange("p o n -> p (o n)")
                    nc.vector.tensor_tensor(xt, psA[:, 2 + i % 2, 0:D], xt, ALU.add).then_inc(S["out_ready"], 1)

                for i in range(CT):
                    norm(0, i)
                    if i >= 2:
                        add(0, i - 2)
                with dve.Fori(1, NJ) as j:
                    for i in range(CT):
                        norm(j, i)
                        if i >= 2:
                            add(j, i - 2)
                        else:
                            add(j - 1, i + 2)
                newton(1, b + 1)
                for i in (2, 3):
                    add(NJ - 1, i)

        @block.tensor
        def _(pe):
            mm = nc.tensor.matmul
            pe.sem_inc(S["xn_transposed"], CREDIT)
            pe.sem_inc(S["ffn_ready"], PAIRED)
            pe.sem_inc(S["parts_transposed"], PAIRED)
            pe.sem_inc(S["pv_done"], CREDIT)
            pe.sem_inc(S["on_transposed"], CREDIT)
            pe.sem_inc(S["wo_done"], CREDIT)
            pe.wait_ge(S["table_in"], 48)
            pe.wait_ge(S["negated"], 1)
            C, SN = range(NT)
            for m, terms in enumerate((((0, C), (1, SN)), ((1, C), (2, SN)))):
                for c in range(KC):
                    for k, (w, f) in enumerate(terms):
                        for d in range(KC):
                            last = mm(psA[:, 2 * m + c, 0:D], wf[:, w, d, c * P:(c + 1) * P], dft_sb[:, f, d, :],
                                      start=(k == 0 and d == 0), stop=(k == 1 and d == KC - 1))
                    last.then_inc(S["t_acc"], 1)
            pe.wait_ge(S["t_copied"], 4)
            for c in range(KC):
                for m, f in enumerate((C, SN)):
                    for d in range(KC):
                        last = mm(psS[:, c, 0:D], tT[:, m, d, c * P:(c + 1) * P], dft_sb[:, f, d, :],
                                  start=(m == 0 and d == 0), stop=(m == 1 and d == KC - 1))
                last.then_inc(S["m_acc"], 1)
            pe.wait_ge(S["m_copied"], 2)
            pe.wait_ge(S["const_ready"], 12)
            pe.wait_ge(S["ones_ready"], 1)
            pe.wait_ge(S["wq_scaled"], 2)
            pe.wait_ge(S["bias_ready"], 3)

            with pe.Fori(0, NB) as b:
                def body(kb, u, do_x, do_qkv, do_t):
                    if do_x:
                        p = b * PAIRS + kb + u
                        pe.wait_ge(S["xn_ready"], 2 * p + 2 + FIRST)
                        pe.wait_ge(S["xnT_ready"], p + CREDIT)
                        for e in range(2):
                            for c in range(KC):
                                last = nc.tensor.transpose(psS[:, e, c * P:(c + 1) * P], xn[:, u % 2, e, c * P:(c + 1) * P], ident[:, :])
                        last.then_inc(S["xn_transposed"], 1)
                    if do_qkv:
                        p = b * PAIRS + kb + u - 1
                        par = (u - 1) % 2
                        pe.wait_ge(S["xnT_ready"], p + 1 + CREDIT)
                        for e in range(2):
                            pe.wait_ge(S["qk_ready"], 2 * p + e + 1)
                            pe.wait_ge(S["v_ready"], 2 * p + e + 1)
                            for c in range(KC):
                                last = mm(psA[:, 2 * e, 0:QKV], xnT[:, par, e, c * P:(c + 1) * P], w_sb[:, c, 0:QKV], start=(c == 0), stop=(c == KC - 1))
                            last.then_inc(S["qkv_ready"], 1)
                            pe.wait_ge(S["ffn_copied"], 2 * p + e + 1)
                            mm(psA[:, 2 * e + 1, 0:D], ones[:, :], bias_p[:, :], start=True, stop=False)
                            for c in range(KC):
                                last = mm(psA[:, 2 * e + 1, 0:D], xnT[:, par, e, c * P:(c + 1) * P], w_sb[:, c, QKV:QKV + D], start=False, stop=(c == KC - 1))
                            last.then_inc(S["ffn_ready"], 1)
                    if do_t:
                        p = b * PAIRS + kb + u - 3
                        par = (u - 3) % 2
                        pe.wait_ge(S["parts_ready"], p + 1 + CREDIT)
                        for e in range(2):
                            pe.wait_ge(S["partsT_ready"], 2 * p + e + 1)
                            for k in range(BLK):
                                last = nc.tensor.transpose(ps_parts[e][:, k * P:(k + 1) * P], parts[:, par, e, k * P:(k + 1) * P], identb[:, :])
                            last.then_inc(S["parts_transposed"], 1)

                def a_scores(v):
                    n, m, _, (heads, i, q) = A_USES[v]
                    g = n % KV
                    w = (i + 1) * P if q == n // KV else CH
                    per = len(heads) // 2
                    if g == 0 and m == 0:
                        pe.wait_ge(S["stacks_in"], (b * NJ + n // KV + 1) * 16 * LOADS + LOADED)
                    pe.wait_ge(S["a_reduced"], b * ALL + v + 1)
                    for k, r in enumerate(heads):
                        last = mm(psA[:, 2 * (v % 2) + k // per, (k % per) * w:(k % per + 1) * w], q_st[0:ROWS, n, r, i * P:(i + 1) * P],
                                  k_st[0:ROWS, g, q * CH:q * CH + w], start=True, stop=not on_pe(n, q))
                        if on_pe(n, q):
                            last = mm(psA[:, 2 * (v % 2) + k // per, (k % per) * w + w - P:(k % per + 1) * w], identb[:, :], maskb[:, :],
                                      start=False, stop=True)
                    last.then_inc(S["a_scores"], 1)

                for k in range(PAIRS + 3):
                    if k == 1:
                        pe.wait_ge(S["out_ready"], b * TILES + CREDIT)
                    body(k - k % 4, k % 4, k < PAIRS, 1 <= k <= PAIRS, k >= 3)
                    if k == PAIRS:
                        for name in ("qk_ready", "v_ready", "ffn_copied"):
                            pe.wait_ge(S[name], (b + 1) * TILES + CREDIT)
                        for v in range(CREDIT):
                            a_scores(v)
                for v in range(CREDIT, PRE):
                    a_scores(v)
                pe.wait_ge(S["partsT_ready"], (b + 1) * TILES + CREDIT)

                def pv(j, g, u):
                    n = step_of(b, j, g)
                    tile, s0, _, banks, diag = units(j)[u]
                    if u == 0:
                        pe.wait_ge(S["o_copied"], n + FIRST)
                    if diag is not None:
                        pe.wait_ge(S["diag_masked"], 4 * n + diag + 1)
                    else:
                        pe.wait_ge(S["probs_ready"], banks_before(b, j, g) + banks + RING)
                    for r in range(R):
                        last = mm(psO[32 * r:32 * r + VW, s0:CH], v_sb[:, tile, g, :], prob[:, u % 2, r, s0:CH],
                                  start=(u == 0), stop=(u == 4 * j + 3), tile_position=(0, 32 * r))
                    last.then_inc(S["pv_done"], 1)

                def one(j, g):
                    n = step_of(b, j, g)
                    nl = n_in_batch(j, g)
                    tail = nl == STEPS - 1
                    v = PRE if nl == 0 else plan[nl - 1][-1]
                    before = banks_before(b, j, g)
                    pe.wait_ge(S["shift_in"], (n + 1) * 16 * CT + LOADED)
                    for u, (tile, s0, count, banks, _) in enumerate(units(j)):
                        hp = R // count
                        w = CH - s0
                        start = v
                        for k in range(count):
                            bank = banks - count + k
                            if not tail or bank < RING:
                                pe.wait_ge(S["probs_ready"], before + bank + 1)
                            elif bank < 5:
                                pe.wait_ge(S["a_reduced"], (b + 1) * ALL + CREDIT)
                            else:
                                pe.wait_ge(S["probs_ready"], before + bank - 1)
                            for h in range(hp):
                                last = mm(score_bank(tail, bank)[:, h * w:(h + 1) * w], k_st[0:ROWS + SHIFT, g, tile * P:(tile + 1) * P],
                                          q_st[0:ROWS + SHIFT, nl, k * hp + h, s0:CH], start=True, stop=True)
                            last.then_inc(S["scores_ready"], 1)
                            masked = units(j)[u - 1][4] is not None if u > 0 else j == 0
                            if k == min(count - 1, PV_LATE if masked or tail else PV_AT):
                                if u > 0:
                                    pv(j, g, u - 1)
                                elif nl > 0:
                                    pv(*((j, g - 1, 4 * j + 3) if g > 0 else (j - 1, KV - 1, 4 * j - 1)))
                            for _ in range(early(plan[nl][u] - start, k)):
                                a_scores(v)
                                v += 1
                        while v < plan[nl][u]:
                            a_scores(v)
                            v += 1
                for n in range(STEPS):
                    one(n // KV, n % KV)
                pv(NJ - 1, KV - 1, TILES - 1)

                pe.wait_ge(S["o_copied"], (b + 1) * STEPS + FIRST)
                pe.wait_ge(S["a_reduced"], (b + 1) * ALL + CREDIT)

                def tr_o(j, i):
                    t = b * TILES + 4 * j + i
                    pe.wait_ge(S["o_normed"], t + 1)
                    for g in range(KV):
                        last = nc.tensor.transpose(psA[:, i % 2, g * P:(g + 1) * P],
                                                   oraw[:, 4 * j + g, i * P:(i + 1) * P], ident[:, :])
                    last.then_inc(S["o_transposed"], 1)

                def tr_n(j, i):
                    t = b * TILES + 4 * j + i
                    pe.wait_ge(S["o_normed"], t + 1 + CREDIT)
                    pe.wait_ge(S["onT_ready"], t + 1)
                    for c in range(KC):
                        last = nc.tensor.transpose(psS[:, i % 2, c * P:(c + 1) * P], o_n[:, i % 2, c * P:(c + 1) * P], ident[:, :])
                    last.then_inc(S["on_transposed"], 1)

                def project(j, i):
                    t = b * TILES + 4 * j + i
                    pe.wait_ge(S["onT_ready"], t + 1 + CREDIT)
                    pe.wait_ge(S["out_ready"], t + 1)
                    for c in range(KC):
                        last = mm(psA[:, 2 + i % 2, 0:D], o_nT[:, i % 2, c * P:(c + 1) * P], wo_sb[:, c, :], start=(c == 0), stop=(c == KC - 1))
                    last.then_inc(S["wo_done"], 1)

                for t in range(TILES + 2):
                    if t < TILES:
                        tr_o(t // CT, t % CT)
                    if 1 <= t <= TILES:
                        tr_n((t - 1) // CT, (t - 1) % CT)
                    if t >= 2:
                        project((t - 2) // CT, (t - 2) % CT)


_INS = ["L0_attn_x", "L0_attn_wq", "L0_attn_wk", "L0_attn_wv", "L0_attn_wo",
        "L0_ffn_w_freq_real", "L0_ffn_w_freq_imag", "L0_ffn_bias"]


def kernel(**inputs):
    import numpy as _np
    import concourse.bacc as _bacc
    from concourse import mybir as _mybir
    from concourse.bass_utils import run_bass_kernel_spmd as _run

    nc = _bacc.Bacc("TRN2", target_bir_lowering=False, num_devices=1)
    arrays, args = {}, []

    def give(name, a):
        arrays[name] = a
        args.append(nc.dram_tensor(name, a.shape, _mybir.dt.from_np(a.dtype), kind="ExternalInput").ap())

    for name in _INS:
        give(f"in_{name}", _np.ascontiguousarray(inputs[name]))
    N = 256
    turn = 2.0 * _np.pi * ((_np.arange(N)[:, None] * _np.arange(N)[None, :]) % N) / N
    give("dft_tables", _np.stack([_np.cos(turn), _np.sin(turn)]).astype(_np.float32))
    inv = (1.0 / _np.float32(10000.0) ** (_np.arange(8, dtype=_np.float32) / _np.float32(8))).astype(_np.float32)
    ang = (_np.arange(2048, dtype=_np.float32)[:, None] * inv[None, :]).astype(_np.float32)
    give("rope_tables", _np.stack([_np.cos(ang), _np.sin(ang)]).astype(_np.float32))
    out = nc.dram_tensor("out_0", (2, 2048, 256), _mybir.dt.float32, kind="ExternalOutput").ap()
    attention_fourier_block(nc, *args, out)
    r = _run(nc, [arrays], core_ids=[0])
    return r.results[0]["out_0"]
```
